# Optimizing a Trainium2 kernel written in Bass

```python
import numpy as np
import jax
import jax.numpy as jnp

def _softmax(x, axis=-1):
    return jax.nn.softmax(x, axis=axis)

def _gelu(x):
    return jax.nn.gelu(x, approximate=True)

def _silu(x):
    return jax.nn.silu(x)

def _sigmoid(x):
    return jax.nn.sigmoid(x)

def _layernorm(x, axis=-1, eps=1e-05):
    m = jnp.mean(x, axis=axis, keepdims=True)
    v = jnp.var(x, axis=axis, keepdims=True)
    return (x - m) / jnp.sqrt(v + eps)

def _scatter_add(tgt, idx, src, axis=0):
    return tgt.at[idx].add(src)

def _segment_sum(src, seg, n):
    return jax.ops.segment_sum(src, seg, n)
kernel_name = 'mk_gnn_resnorm_d1_gnn_r8_137008'

def setup_inputs(seed: int=0):
    np.random.seed(seed)
    _w = jnp.asarray

    def _rec_inputs():
        import jax
        import jax.numpy as jnp
        _gk = jax.random.key(seed)
        x = -0.0006008 + 1.001 * jax.random.normal(jax.random.fold_in(_gk, 1), (6250, 128), jnp.float32)
        src = jax.random.randint(jax.random.fold_in(_gk, 2), (100000,), 0, 6250, jnp.int32)
        dst = jax.random.randint(jax.random.fold_in(_gk, 3), (100000,), 0, 6250, jnp.int32)
        _o = jnp.argsort(dst, stable=True)
        src = src[_o]
        dst = dst[_o]
        edge_type_32 = jax.random.randint(jax.random.fold_in(_gk, 12), (100000,), 0, 32, jnp.int32)
        node_type_16 = jax.random.randint(jax.random.fold_in(_gk, 13), (6250,), 0, 16, jnp.int32)
        return (x, src, dst, edge_type_32, node_type_16)
    x, src, dst, edge_type_32, node_type_16 = _rec_inputs()

    def _L0_gnn_setup():
        import jax, jax.numpy as jnp
        import numpy as np
        N = 2500
        E = 40000
        DIN = 128
        HID = 128
        H = 8
        HS = HID // H
        NT = 16
        RT = 32
        L = 2
        OUT = 128
        SQRT_D = float(np.sqrt(HS))

        def typed_linear(x, t, W):
            y_all = jnp.einsum('nd,tdo->nto', x, W)
            return jnp.take_along_axis(y_all, t[:, None, None], axis=1)[:, 0]

        def edge_softmax(a, dst, n):
            amax = jax.ops.segment_max(a, dst, num_segments=n)
            ex = jnp.exp(a - amax[dst])
            s = jax.ops.segment_sum(ex, dst, num_segments=n)
            return ex / s[dst]

        def gt_layer(x, ntype, etype, src, dst, Wk, Wq, Wv, Wa, Watt, Wmsg, pri, skip, g, b):
            n = x.shape[0]
            k = typed_linear(x, ntype, Wk).reshape(n, H, HS)
            q = typed_linear(x, ntype, Wq).reshape(n, H, HS)
            v = typed_linear(x, ntype, Wv).reshape(n, H, HS)
            kT = jnp.einsum('nhd,htdo->nhto', k, Watt)
            vT = jnp.einsum('nhd,htdo->nhto', v, Wmsg)
            kw = kT[src, :, etype]
            m = vT[src, :, etype]
            a = jnp.einsum('ehd,ehd->eh', kw, q[dst]) * pri[:, etype].T / SQRT_D
            att = edge_softmax(a, dst, n)
            msg = (m * att[:, :, None]).reshape(-1, H * HS)
            hag = jax.ops.segment_sum(msg, dst, num_segments=n)
            h = jax.nn.silu(typed_linear(hag, ntype, Wa))
            alpha = jax.nn.sigmoid(skip[ntype])[:, None]
            h = h * alpha + x * (1.0 - alpha)
            mu = jnp.mean(h, axis=-1, keepdims=True)
            var = jnp.mean((h - mu) ** 2, axis=-1, keepdims=True)
            return (h - mu) * jax.lax.rsqrt(var + 1e-05) * g + b
        key = jax.random.key(seed)
        ks = jax.random.split(key, 16)
        f32 = jnp.float32
        return {'x': jax.random.normal(ks[0], (N, DIN), f32), 'ntype': jax.random.randint(ks[1], (N,), 0, NT), 'etype': jax.random.randint(ks[2], (E,), 0, RT), 'src': jax.random.randint(ks[3], (E,), 0, N), 'dst': jax.random.randint(ks[4], (E,), 0, N), 'Wk': jax.random.normal(ks[5], (L, NT, DIN, HID), f32) / np.sqrt(DIN), 'Wq': jax.random.normal(ks[6], (L, NT, DIN, HID), f32) / np.sqrt(DIN), 'Wv': jax.random.normal(ks[7], (L, NT, DIN, HID), f32) / np.sqrt(DIN), 'Wa': jax.random.normal(ks[8], (L, NT, HID, HID), f32) / np.sqrt(HID), 'Watt': jax.random.normal(ks[9], (L, H, RT, HS, HS), f32) / np.sqrt(HS), 'Wmsg': jax.random.normal(ks[10], (L, H, RT, HS, HS), f32) / np.sqrt(HS), 'pri': jnp.ones((L, H, RT), f32), 'skip': jnp.ones((L, NT), f32), 'ln_g': jnp.ones((L, HID), f32), 'ln_b': jnp.zeros((L, HID), f32), 'ff_w': jax.random.normal(ks[11], (HID, OUT), f32) / np.sqrt(HID), 'ff_b': jnp.zeros((OUT,), f32)}
    _L0_gnn_all = _L0_gnn_setup()
    _L0_gnn_in = {k: v for k, v in _L0_gnn_all.items() if k in ('Wk', 'Wq', 'Wv', 'Wa', 'Watt', 'Wmsg', 'pri', 'skip', 'ln_g', 'ln_b', 'ff_w', 'ff_b')}
    del _L0_gnn_all
    return {'x': x, 'src': src, 'dst': dst, 'edge_type_32': edge_type_32, 'node_type_16': node_type_16, 'L0_gnn_Wk': _L0_gnn_in['Wk'], 'L0_gnn_Wq': _L0_gnn_in['Wq'], 'L0_gnn_Wv': _L0_gnn_in['Wv'], 'L0_gnn_Wa': _L0_gnn_in['Wa'], 'L0_gnn_Watt': _L0_gnn_in['Watt'], 'L0_gnn_Wmsg': _L0_gnn_in['Wmsg'], 'L0_gnn_pri': _L0_gnn_in['pri'], 'L0_gnn_skip': _L0_gnn_in['skip'], 'L0_gnn_ln_g': _L0_gnn_in['ln_g'], 'L0_gnn_ln_b': _L0_gnn_in['ln_b'], 'L0_gnn_ff_w': _L0_gnn_in['ff_w'], 'L0_gnn_ff_b': _L0_gnn_in['ff_b']}

def reference(x, src, dst, edge_type_32, node_type_16, L0_gnn_Wk, L0_gnn_Wq, L0_gnn_Wv, L0_gnn_Wa, L0_gnn_Watt, L0_gnn_Wmsg, L0_gnn_pri, L0_gnn_skip, L0_gnn_ln_g, L0_gnn_ln_b, L0_gnn_ff_w, L0_gnn_ff_b):
    import jax
    import jax.numpy as jnp

    def _L0_gnn_ref(x, ntype, etype, src, dst, Wk, Wq, Wv, Wa, Watt, Wmsg, pri, skip, ln_g, ln_b, ff_w, ff_b):
        import jax, jax.numpy as jnp
        import numpy as np
        N = 2500
        E = 40000
        DIN = 128
        HID = 128
        H = 8
        HS = HID // H
        NT = 16
        RT = 32
        L = 2
        OUT = 128
        SQRT_D = float(np.sqrt(HS))

        def typed_linear(x, t, W):
            y_all = jnp.einsum('nd,tdo->nto', x, W)
            return jnp.take_along_axis(y_all, t[:, None, None], axis=1)[:, 0]

        def edge_softmax(a, dst, n):
            amax = jax.ops.segment_max(a, dst, num_segments=n)
            ex = jnp.exp(a - amax[dst])
            s = jax.ops.segment_sum(ex, dst, num_segments=n)
            return ex / s[dst]

        def gt_layer(x, ntype, etype, src, dst, Wk, Wq, Wv, Wa, Watt, Wmsg, pri, skip, g, b):
            n = x.shape[0]
            k = typed_linear(x, ntype, Wk).reshape(n, H, HS)
            q = typed_linear(x, ntype, Wq).reshape(n, H, HS)
            v = typed_linear(x, ntype, Wv).reshape(n, H, HS)
            kT = jnp.einsum('nhd,htdo->nhto', k, Watt)
            vT = jnp.einsum('nhd,htdo->nhto', v, Wmsg)
            kw = kT[src, :, etype]
            m = vT[src, :, etype]
            a = jnp.einsum('ehd,ehd->eh', kw, q[dst]) * pri[:, etype].T / SQRT_D
            att = edge_softmax(a, dst, n)
            msg = (m * att[:, :, None]).reshape(-1, H * HS)
            hag = jax.ops.segment_sum(msg, dst, num_segments=n)
            h = jax.nn.silu(typed_linear(hag, ntype, Wa))
            alpha = jax.nn.sigmoid(skip[ntype])[:, None]
            h = h * alpha + x * (1.0 - alpha)
            mu = jnp.mean(h, axis=-1, keepdims=True)
            var = jnp.mean((h - mu) ** 2, axis=-1, keepdims=True)
            return (h - mu) * jax.lax.rsqrt(var + 1e-05) * g + b
        h = x
        for l in range(L):
            h = gt_layer(h, ntype, etype, src, dst, Wk[l], Wq[l], Wv[l], Wa[l], Watt[l], Wmsg[l], pri[l], skip[l], ln_g[l], ln_b[l])
        return h @ ff_w + ff_b
    x = _layernorm(x + _L0_gnn_ref(x, node_type_16, edge_type_32, src, dst, L0_gnn_Wk, L0_gnn_Wq, L0_gnn_Wv, L0_gnn_Wa, L0_gnn_Watt, L0_gnn_Wmsg, L0_gnn_pri, L0_gnn_skip, L0_gnn_ln_g, L0_gnn_ln_b, L0_gnn_ff_w, L0_gnn_ff_b), axis=-1)
    return x

_drawn_inputs = setup_inputs


def setup_inputs(seed=0):
    import zlib

    import numpy as np

    out = dict(_drawn_inputs(seed))
    spreads = {'L0_gnn_pri': (1.0, 0.2),
     'L0_gnn_skip': (1.0, 0.2),
     'L0_gnn_ln_g': (1.0, 0.2),
     'L0_gnn_ln_b': (0.0, 0.1),
     'L0_gnn_ff_b': (0.0, 0.1)}
    factors = {}
    for name, (base, spread) in spreads.items():
        noise = np.random.default_rng([zlib.crc32(name.encode()), seed]).standard_normal(out[name].shape)
        drawn = base * np.exp(spread * noise) if base else spread * noise
        out[name] = jnp.asarray(drawn.astype(out[name].dtype))
    for name, factor in factors.items():
        out[name] = (out[name] * factor).astype(out[name].dtype)
    return out
```

```python
import numpy as np
import concourse.bass as bass
from concourse import mybir
from contextlib import ExitStack

P = 128
N, E, D, H, HS, RT, NT, L = 6250, 100000, 128, 8, 16, 32, 16, 2
NTILES = -(-N // P)
NPAD = NTILES * P
SORTED_TILES = NTILES - 1 + NT
GROUP = 4
GROUPS = SORTED_TILES // GROUP
EPP = -(-E // P)
ETILES = EPP
EROWS = ETILES + 2
BLOCK = 32
NBLOCKS = -(-(ETILES + NTILES - 1) // BLOCK)
SLOTS = NBLOCKS * BLOCK
SCOLS = -(-SLOTS // P)
CHUNKS = P // H
PER_CHUNK = BLOCK // CHUNKS
CLEN = PER_CHUNK * P
QUAD = 4
QPB = BLOCK // QUAD
NQUADS = NBLOCKS * QPB
FIRST_WEIGHED = 4
FIRST_SUMMED = FIRST_WEIGHED + 1
BIG = 1.0e30
NO_NODE = 8192.0
NO_DST = 20000.0
EPS = 1e-5
X_PART = [0, 0, 0, 1, 1, 1, 2, 2]
W_PART = [0, 1, 2, 0, 1, 2, 0, 1]
PARTS = len(X_PART)
TABLE_ROW = 2 * D
RHS0 = D - H
SUMC = H + D


def gnn_kernel(nc, x, src, dst, etype, ntype, Wk, Wq, Wv, Wa, Watt, Wmsg, pri, skip, ln_g, ln_b, ff_w, ff_b, out):
    F32, I32, BF16 = mybir.dt.float32, mybir.dt.int32, mybir.dt.bfloat16
    ALU, ACT, AX = mybir.AluOpType, mybir.ActivationFunctionType, mybir.AxisListType
    PE_, DVE_ = mybir.EngineType.PE, mybir.EngineType.DVE

    ctx = ExitStack()
    with ctx:
        def sb(name, shape, dt):
            return ctx.enter_context(nc.sbuf_tensor(name, shape, dt))

        def sem(name):
            return ctx.enter_context(nc.semaphore(name))

        def dram(name, shape, dt):
            return nc.dram_tensor(name, shape, dt).ap()

        def bc(ap, axis, n):
            u = ap.unsqueeze(axis)
            shape = list(u.shape)
            shape[axis] = n
            return u.to_broadcast(shape)

        table = dram("relation_table", [NPAD * RT, TABLE_ROW], F32)
        qkv_dram = dram("qkv_rows", [NPAD, 3 * D], F32)
        agg_dram = dram("aggregated_rows", [NPAD, D], F32)
        x_sorted = dram("x_sorted", [SORTED_TILES * P, D], F32)
        h_sorted = dram("h_sorted", [SORTED_TILES * P, D], F32)
        node_of_place = dram("node_of_place", [P * SORTED_TILES, 1], I32)
        key_flat = dram("edge_keys", [EROWS * P], F32)
        dst_flat = dram("edge_dst", [EROWS * P + 2], F32)
        edge_rows = dram("edge_rows", [EROWS, 4 * P], F32)
        flag_rows = dram("segment_flags", [2, SCOLS * P, P], F32)
        w_parts = dram("relation_weight_parts", [L, 2, 3, H, HS, RT * HS], BF16)

        ident = sb("ident", [P, P], F32)
        identb = sb("identb", [P, P], BF16)
        ones = sb("ones", [P, P], F32)
        iota_free = sb("iota_free", [P, P], F32)
        key_of = sb("key_of", [P, SCOLS * P], F32)
        minus_dst = sb("minus_dst", [P, SCOLS * P], F32)
        invalid = sb("invalid", [P, SCOLS * P], F32)
        crossing = sb("crossing", [1, SCOLS * P // BLOCK], F32)
        dst_tile = sb("dst_tile", [1, SCOLS * P], I32)
        gather_node = sb("gather_node", [P, SORTED_TILES], I32)
        scatter_node = sb("scatter_node", [P, SORTED_TILES], I32)
        tile_type = sb("tile_type", [1, SORTED_TILES], I32)
        type_of_tile = sb("type_of_tile", [P, SORTED_TILES], F32)
        half_alpha = sb("half_alpha", [P, SORTED_TILES], F32)
        one_less_alpha = sb("one_less_alpha", [P, SORTED_TILES], F32)
        alpha_t = sb("alpha_t", [P, NT], F32)
        type_no = sb("type_no", [P, NT], F32)
        row_const = sb("row_const", [P, 3, D], F32)
        minus_half = sb("minus_half", [P, GROUP], F32)

        sums = sb("sums", [P, NTILES, SUMC], F32)
        region_q = sb("region_q", [P, NTILES * 3 * D], BF16)
        region_a = sb("region_a", [P, 2 * BLOCK * TABLE_ROW], F32)
        region_b = sb("region_b", [P, 2 * BLOCK * P], F32)

        q_parts = region_q[:, :].rearrange("p (c k d) -> p c k d", c=NTILES, k=3)
        wqf = region_q[:, :].bitcast(F32)
        w_qkv = wqf[:, 0:NT * 3 * D].rearrange("p (t n) -> p t n", t=NT)
        w_a = wqf[:, NT * 3 * D:NT * 3 * D + NT * D].rearrange("p (t n) -> p t n", t=NT)
        w_ff = wqf[:, NT * 4 * D:NT * 4 * D + D]

        rows = region_a[:, :].rearrange("p (r s n) -> p r s n", r=2, s=BLOCK)
        onehots = region_b[:, :].rearrange("p (r s n) -> p r s n", r=2, s=BLOCK)

        stage = region_a[:, :].rearrange("p (r t n) -> p r t n", r=2, t=RT)
        rb16 = region_b[:, :].bitcast(BF16)
        spare = sums[:, :].rearrange("p c n -> p (c n)")
        kvq = spare[:, 0:12 * D].rearrange("p (r n) -> p r n", r=4)
        resid1, resid2 = spare[:, 12 * D:15 * D], spare[:, 15 * D:18 * D]
        rel_f = spare[:, 0:L * 1024].rearrange("p (l n) -> p l n", l=L)
        rel_r = spare[:, 2048:3072]
        rel_p = spare[:, 3072:6144].bitcast(BF16).rearrange("p (l k w n) -> p l k w n", l=L, k=2, w=3)
        rel_pri = spare[:, 6144:6208].rearrange("p (l t) -> p l t", l=L)
        w_rel = rb16[:, 0:8192].rearrange("p (k n) -> p k n", k=2 * H)
        x_spread = rb16[:, 8192:12288].rearrange("p (r k w d) -> p r k w d", r=2, k=2 * H, w=PARTS)
        x_spreadT = rb16[:, 12288:16384].rearrange("p (r k n) -> p r k n", r=2, k=2 * H)

        def take(base, w, shape):
            v = region_a[:, base:base + w]
            return v.rearrange("p (r a b) -> p r a b", r=2, a=shape[0]), base + w

        o = 0
        g_in, o = take(o, 2 * GROUP * D, (GROUP, D))
        g_res, o = take(o, 2 * GROUP * D, (GROUP, D))
        g_x, o = take(o, 2 * GROUP * D, (GROUP, D))
        g_inT, o = take(o, 2 * GROUP * D, (GROUP, D))
        g_th, o = take(o, 2 * GROUP * D, (GROUP, D))
        g_h, o = take(o, 2 * GROUP * D, (GROUP, D))
        g_hn, o = take(o, 2 * GROUP * D, (GROUP, D))
        g_hnT, o = take(o, 2 * GROUP * D, (GROUP, D))
        g_out, o = take(o, 2 * GROUP * 3 * D, (GROUP, 3 * D))
        tile_is_type = region_a[:, o:o + SORTED_TILES * NT].rearrange("p (i t) -> p i t", t=NT)
        junk2 = sb("junk2", [1, 1], F32)
        bn_in = sb("bn_in", [P, 2, GROUP, 6], F32)
        mean_var = sb("mean_var", [P, 2, GROUP, 2], F32)
        var_eps = sb("var_eps", [P, 2, GROUP], F32)
        rstd = sb("rstd", [P, 2, GROUP], F32)

        block_keys = sb("block_keys", [P, 2, BLOCK], I32)
        onehotT = sb("onehotT", [P, 2, QUAD, P], BF16)
        prod = sb("prod", [P, 2, QUAD, D], F32)
        score = sb("score", [P, 2, BLOCK, H], F32)
        masked = sb("masked", [P, PER_CHUNK, CHUNKS, H], F32)
        flags = sb("flags", [P, 2, 2, CLEN], F32)
        first_seg = sb("first_seg", [P, CLEN], F32)
        last_seg = sb("last_seg", [P, CLEN], F32)
        fwd = sb("fwd", [P, CLEN], F32)
        bwd = sb("bwd", [P, CLEN], F32)
        edge_max = sb("edge_max", [P, CLEN], F32)
        below_max = sb("below_max", [P, BLOCK, H], F32)
        carry_in = sb("carry_in", [1, 2, 2, H, CHUNKS + 1], F32)
        carry_out = sb("carry_out", [1, 2, H, CHUNKS + 1], F32)
        carry_rows = sb("carry_rows", [1, 2, CHUNKS, H], F32)
        chunk_carry = sb("chunk_carry", [P, 2], F32)
        carried = sb("carried", [1, H], F32)
        lower = sb("lower", [1, H], F32)
        cross_hot = sb("cross_hot", [1, P], F32)
        rescale = sb("rescale", [P, H], F32)
        recip = prod[:, :].rearrange("p r s d -> p (r s d)")[:, 0:NTILES * H].rearrange("p (c h) -> p c h", h=H)

        bank = [ctx.enter_context(nc.psum_tensor(f"bank{i}", [P, 512], F32)) for i in range(8)]

        pool_const = sem("pool_const")
        pool_chain = sem("pool_chain")
        dve_chain = sem("dve_chain")
        pads_set = sem("pads_set")
        type_in, edge_in = sem("type_in"), sem("edge_in")
        counted, placed_psum = sem("counted"), sem("placed_psum")
        place_ready, place_init, place_done = sem("place_ready"), sem("place_init"), sem("place_done")
        place_loaded = sem("place_loaded")
        flat_ready, flat_stored, rows_built = sem("flat_ready"), sem("flat_stored"), sem("rows_built")
        bound_counted, bound_psum = sem("bound_counted"), sem("bound_psum")
        slot_rows_ready, slot_rows_in = sem("slot_rows_ready"), sem("slot_rows_in")
        slot_calc, slot_T, slot_copied, flags_stored = sem("slot_calc"), sem("slot_T"), sem("slot_copied"), sem("flags_stored")
        prep_done = sem("prep_done")
        layer_const_in, alpha_exp, layer_const_ready = sem("layer_const_in"), sem("alpha_exp"), sem("layer_const_ready")
        weights_in = sem("weights_in")
        rel_in, rel_split, parts_stored, w_rel_in = sem("rel_in"), sem("rel_split"), sem("parts_stored"), sem("w_rel_in")
        pad_rows_stored = sem("pad_rows_stored")
        gathered = [sem(f"gathered{i}") for i in range(2)]
        res_in = [sem(f"res_in{i}") for i in range(2)]
        stored = [sem(f"stored{i}") for i in range(2)]
        scattered = [sem(f"scattered{i}") for i in range(2)]
        inT_psum, inT_ready, z_psum, tanh_done = sem("inT_psum"), sem("inT_ready"), sem("z_psum"), sem("tanh_done")
        var_ready, rstd_ready, hn_ready = sem("var_ready"), sem("rstd_ready"), sem("hn_ready")
        hnT_psum, hnT_ready, out_psum, out_ready = sem("hnT_psum"), sem("hnT_ready"), sem("out_psum"), sem("out_ready")
        kvq_in = [sem(f"kvq_in{i}") for i in range(4)]
        spread_ready, spread_T, spreadT_ready = sem("spread_ready"), sem("spread_T"), sem("spreadT_ready")
        table_psum, stage_act, stage_dve = sem("table_psum"), sem("stage_act"), sem("stage_dve")
        table_stored = [sem(f"table_stored{i}") for i in range(2)]
        rows_in = [sem(f"rows_in{i}") for i in range(QPB)]
        onehot_ready, onehotT_psum, onehotT_ready = sem("onehot_ready"), sem("onehotT_psum"), sem("onehotT_ready")
        q_psum, prod_ready, score_ready = sem("q_psum"), sem("prod_ready"), sem("score_ready")
        flags_in = [sem(f"flags_in{i}") for i in range(2)]
        masked_ready, masked_T, scans_ready = sem("masked_ready"), sem("masked_T"), sem("scans_ready")
        chunk_rows, carry_ready, carry_T, max_ready, max_T = (sem("chunk_rows"), sem("carry_ready"), sem("carry_T"),
                                                              sem("max_ready"), sem("max_T"))
        below_ready, exp_ready, lower_ready, rescale_psum = (sem("below_ready"), sem("exp_ready"), sem("lower_ready"),
                                                             sem("rescale_psum"))
        cross_ready = sem("cross_ready")
        weighted, sum_psum, sum_added = sem("weighted"), sem("sum_psum"), sem("sum_added")
        z_used, var2_ready, rstd2_ready = sem("z_used"), sem("var2_ready"), sem("rstd2_ready")
        act_chain, q_split = sem("act_chain"), sem("q_split")
        keys_ready, passed = sem("keys_ready"), sem("passed")
        agg_ready, agg_stored = sem("agg_ready"), sem("agg_stored")

        pa = region_a
        src_i = pa[:, 0:EPP].bitcast(I32)
        typ_i = pa[:, 800:800 + EPP].bitcast(I32)
        dst_i = pa[:, 1600:1600 + EPP].bitcast(I32)
        key_f = pa[:, 2400:2400 + EPP]
        dst_f = pa[:, 3200:3200 + EPP]
        junk = pa[:, 4000:4000 + EPP]
        junk_b = pa[:, 14000:14000 + EPP]
        bounds = pa[:, 4800:4800 + NTILES - 1]
        starts = pa[:, 4864:4864 + NTILES - 1]
        starts_i = pa[:, 4928:4928 + NTILES - 1].bitcast(I32)
        slot_cmp = pa[:, 5000:5000 + SCOLS * (NTILES - 1)].rearrange("p (c d) -> p c d", c=SCOLS)
        slot_no = pa[:, 5400:5400 + SCOLS]
        slot_dt = pa[:, 5408:5408 + SCOLS]
        slot_et = pa[:, 5416:5416 + SCOLS]
        slot_et_i = pa[:, 5424:5424 + SCOLS].bitcast(I32)
        slot_base = pa[:, 5432:5432 + SCOLS]
        cross_col = pa[:, 5440:5440 + SCOLS]
        pad_lo = pa[:, 5500:5500 + 2]
        srow = pa[:, 5632:5632 + SCOLS * 512].rearrange("p (c k e) -> p c k e", c=SCOLS, k=4)
        s_loc = pa[:, 9216:9216 + SCOLS * P].rearrange("p (c e) -> p c e", c=SCOLS)
        s_valid = pa[:, 10112:10112 + SCOLS * P].rearrange("p (c e) -> p c e", c=SCOLS)
        s_a = pa[:, 11008:11008 + SCOLS * P].rearrange("p (c e) -> p c e", c=SCOLS)
        s_flag = pa[:, 11904:11904 + 2 * SCOLS * P].rearrange("p (k c e) -> p k c e", k=2, c=SCOLS)
        pb = region_b
        upper = pb[:, 0:P]
        iota_i = pb[:, 128:256].bitcast(I32)
        part_i = pb[:, 256:257].bitcast(I32)
        part_f = pb[:, 257:258]
        slot_i = pb[:, 264:264 + SCOLS].bitcast(I32)
        node_i = pb[:, 272:272 + NTILES].bitcast(I32)
        nt_i = pb[:, 328:328 + NTILES].bitcast(I32)
        nt_f = pb[:, 384:384 + NTILES]
        onehot_t = pb[:, 512:512 + NT * NTILES].rearrange("p (t c) -> p t c", t=NT)
        keep = pb[:, 1300:1300 + NT * NTILES].rearrange("p (t c) -> p t c", t=NT)
        ranks = pb[:, 2100:2100 + NT * NTILES].rearrange("p (t c) -> p t c", t=NT)
        tot = pb[:, 2900:2916]
        tot_i = pb[:, 2916:2932].bitcast(I32)
        tiles_t = pb[:, 2932:2948]
        first_tile = pb[:, 2948:2964]
        base_t = pb[:, 2964:2980]
        pos = pb[:, 2980:2980 + NTILES]
        pos_i = pb[:, 3032:3032 + NTILES].bitcast(I32)
        pos_lo = pb[:, 3084:3084 + NTILES].bitcast(I32)
        pos_hi = pb[:, 3136:3136 + NTILES].bitcast(I32)
        pos_lof = pb[:, 3188:3188 + NTILES]
        is_pad = pb[:, 3240:3240 + NTILES]
        place_i = pb[:, 3292:3292 + NTILES].bitcast(I32)
        no_node = pb[:, 3344:3344 + SORTED_TILES].bitcast(I32)
        tile_no = pb[:, 3408:3408 + SORTED_TILES]
        type_f = pb[:, 3472:3472 + SORTED_TILES]
        type_cmp = pb[:, 3584:3584 + SORTED_TILES * NT].rearrange("p (i t) -> p i t", t=NT)
        zeros = pb[:, 4608:4608 + 3 * D]
        pad_dst = pb[:, 5000:5002]
        pad_key = pb[:, 5004:5006]
        before_first = pb[:, 5008:5009]
        node_f = pb[:, 5016:5016 + SORTED_TILES]
        ALL_FULL = E // EPP
        LAST_EDGES = E - ALL_FULL * EPP
        NFULL = N // NTILES
        LAST_NODES = N - NFULL * NTILES

        block = ctx.enter_context(nc.Block())

        def late_quad(b, par, q, first):
            return (b - 1, 1 - par, q - first) if q >= first else (b - 2, par, q - first + QPB)

        def is_block(b):
            return not isinstance(b, int) or 0 <= b < NBLOCKS

        def wait(eng, semaphore, value):
            if not (isinstance(value, int) and value <= 0):
                eng.wait_ge(semaphore, value)

        class Chain:

            def __init__(self, eng, semaphore):
                self.eng, self.semaphore, self.n = eng, semaphore, 0

            def step(self, instruction):
                instruction.then_inc(self.semaphore, 1)
                self.n = self.n + 1
                return self.n

            def wait(self, upto=None):
                self.eng.wait_ge(self.semaphore, self.n if upto is None else upto)

        def repeat(eng, count, body, chain=None):
            start = chain.n if chain else 0
            body(0)
            per = (chain.n - start) if chain else 0
            if count > 1:
                with eng.Fori(1, count) as i:
                    if chain:
                        chain.n = i * per + start
                    body(i)
                if chain:
                    chain.n = start + per * count

        def group_rows(array, g):
            return array[bass.ds(g * GROUP * P, GROUP * P), :].rearrange("(t p) d -> p t d", p=P)

        HALF_GROUPS = GROUPS // 2
        FOURS = NTILES // 4

        def stage_uses(l, i, k):
            return 2 * i + (k // 2 + l * (NTILES // 2 + 1 - k % 2))

        def kvq_uses(l, i, k):
            return i + l * (FOURS + (k == 0))

        @block.sync
        def _(sp):
            sp.wait_ge(pads_set, 1)
            sp.dma_start(nt_i[0:NFULL, :], ntype[0:NFULL * NTILES].rearrange("(p c) -> p c", c=NTILES)).then_inc(type_in, 16)
            sp.dma_start(nt_i[NFULL:P, 0:LAST_NODES], ntype[NFULL * NTILES:N].unsqueeze(0)).then_inc(type_in, 16)
            for buf, source in ((src_i, src), (typ_i, etype), (dst_i, dst)):
                sp.dma_start(buf[0:ALL_FULL, :], source[0:ALL_FULL * EPP].rearrange("(p c) -> p c", c=EPP)).then_inc(edge_in, 16)
                sp.dma_start(buf[ALL_FULL:P, 0:LAST_EDGES], source[ALL_FULL * EPP:E].unsqueeze(0)).then_inc(edge_in, 16)
            sp.dma_start(node_of_place.rearrange("(p i) o -> p (i o)", p=P), no_node).then_inc(place_init, 16)
            sp.dma_start(qkv_dram[N:NPAD, :], zeros[0:NPAD - N, :]).then_inc(pad_rows_stored, 16)
            sp.dma_start(dst_flat[0:1].unsqueeze(0), before_first[0:1, :]).then_inc(flat_stored, 16)
            sp.dma_start(dst_flat[1 + P * EPP:1 + EROWS * P].rearrange("(p c) -> p c", c=2), pad_dst).then_inc(flat_stored, 16)
            sp.dma_start(dst_flat[1 + EROWS * P:2 + EROWS * P].unsqueeze(0), pad_dst[0:1, 0:1]).then_inc(flat_stored, 16)
            sp.dma_start(key_flat[P * EPP:EROWS * P].rearrange("(p c) -> p c", c=2), pad_key).then_inc(flat_stored, 16)
            sp.wait_ge(flat_ready, 1)
            sp.dma_start(key_flat[0:P * EPP].rearrange("(p c) -> p c", c=EPP), key_f).then_inc(flat_stored, 16)
            sp.dma_start(dst_flat[1:1 + P * EPP].rearrange("(p c) -> p c", c=EPP), dst_f).then_inc(flat_stored, 16)
            sp.wait_ge(flat_stored, 96)
            for k, flat in enumerate((key_flat[0:EROWS * P], dst_flat[1:1 + EROWS * P], dst_flat[0:EROWS * P],
                                      dst_flat[2:2 + EROWS * P])):
                sp.dma_start(edge_rows[:, k * P:(k + 1) * P], flat.rearrange("(r e) -> r e", e=P)).then_inc(rows_built, 16)
            sp.wait_ge(place_done, 16 * NTILES)
            sp.dma_start(scatter_node[:, :], node_of_place.rearrange("(p i) o -> p (i o)", p=P)).then_inc(place_loaded, 16)
            sp.wait_ge(slot_calc, 1)
            for k in range(2):
                sp.dma_start(flag_rows[k].rearrange("(c p) e -> p c e", p=P), s_flag[:, k]).then_inc(flags_stored, 16)
            sp.wait_ge(flags_stored, 32)
            sp.wait_ge(rel_split, L)
            for l in range(L):
                for k in range(2):
                    for w in range(3):
                        sp.dma_start(w_parts[l, k, w].rearrange("h d n -> (h d) n"), rel_p[:, l, k, w, :]).then_inc(parts_stored, 16)
            sp.wait_ge(parts_stored, 16 * 6 * L)
            sp.wait_ge(prep_done, 1)

            def relation_weights(l):
                for k in range(2):
                    for s in range(PARTS):
                        sp.dma_start(w_rel[s * HS:(s + 1) * HS, k * H:(k + 1) * H, :],
                                     w_parts[l, k, W_PART[s]].rearrange("h d n -> d h n")).then_inc(w_rel_in, 16)

            def typed(ph):
                if ph > 0:
                    for half in (slice(0, NT // 2), slice(NT // 2, NT)):
                        sp.dma_start(w_a[:, half, :], Wa[ph - 1, half].rearrange("t d o -> d t o")).then_inc(weights_in, 16)
                    sp.dma_start(row_const[:, 0, :], ln_g[ph - 1:ph, :].to_broadcast([P, D])).then_inc(layer_const_in, 16)
                    sp.dma_start(row_const[:, 1, :], ln_b[ph - 1:ph, :].to_broadcast([P, D])).then_inc(layer_const_in, 16)
                    sp.dma_start(row_const[:, 2, :], ff_b.unsqueeze(0).to_broadcast([P, D])).then_inc(layer_const_in, 16)
                    sp.dma_start(alpha_t[:, :], skip[ph - 1:ph, :].to_broadcast([P, NT])).then_inc(layer_const_in, 16)
                if ph < 2:
                    for k, w in enumerate((Wq, Wk, Wv)):
                        for half in (slice(0, NT // 2), slice(NT // 2, NT)):
                            sp.dma_start(w_qkv[:, half, k * D:(k + 1) * D], w[ph, half].rearrange("t d o -> d t o")).then_inc(weights_in, 16)
                else:
                    sp.dma_start(w_ff, ff_w).then_inc(weights_in, 16)
                if ph < 2:
                    relation_weights(ph)

                def load(i, par):
                    g = 2 * i + par
                    sp.dma_start(g_res[:, par], group_rows(x_sorted if ph == 1 else h_sorted, g)).then_inc(res_in[par], 16)
                    if ph == 2:
                        sp.dma_start(g_x[:, par], group_rows(x_sorted, g)).then_inc(res_in[par], 16)

                if ph > 0:
                    load(0, 0)
                    load(0, 1)

                def groups(i):
                    for par in range(2):
                        g = 2 * i + par
                        if ph == 0:
                            sp.wait_ge(gathered[par], i * 64 + 64)
                            sp.dma_start(group_rows(x_sorted, g), g_hn[:, par]).then_inc(stored[par], 16)
                        if ph == 1:
                            sp.wait_ge(hn_ready, g + 1)
                            sp.dma_start(group_rows(h_sorted, g), g_hn[:, par]).then_inc(stored[par], 16)
                        if ph == 2:
                            sp.wait_ge(out_ready, g + 2 * GROUPS + 1)
                        if ph > 0 and not (isinstance(i, int) and i == HALF_GROUPS - 1):
                            load(i + 1, par)

                repeat(sp, HALF_GROUPS - 1, groups)
                groups(HALF_GROUPS - 1)

            def build_table(l):
                for par in range(2):
                    sp.wait_ge(scattered[par], 64 * HALF_GROUPS * (l + 1))
                    sp.wait_ge(stored[par], 16 * HALF_GROUPS * (l + 1))
                if l == 0:
                    sp.wait_ge(pad_rows_stored, 16)

                def load(i, k):
                    sp.dma_start(kvq[:, k], qkv_dram[bass.ds((4 * i + k) * P, P), :]).then_inc(kvq_in[k], 16)

                def tile(i, k, more):
                    c = 4 * i + k
                    sp.wait_ge(stage_act, c * H + (l * NTILES + 1) * H)
                    sp.wait_ge(stage_dve, c * H + (l * NTILES + 1) * H)
                    sp.dma_start(table[bass.ds(c * P * RT, P * RT), :].rearrange("(p t) n -> p t n", t=RT),
                                 stage[:, k % 2]).then_inc(table_stored[k % 2], 16)
                    if more:
                        load(i + 1, k)

                for k in range(4):
                    load(0, k)

                def four(i):
                    for k in range(4):
                        tile(i, k, True)

                repeat(sp, FOURS - 1, four)
                for k in range(4):
                    tile(FOURS - 1, k, k == 0)
                tile(FOURS, 0, False)

            def attend(l):
                def load_flags(i, par):
                    for k in range(2):
                        for h in range(1):
                            rows_ = flag_rows[k, bass.ds((2 * i + par) * BLOCK, BLOCK), :]
                            source = bc(rows_.rearrange("(j i) e -> j (i e)", i=PER_CHUNK), 1, H)
                            sp.dma_start(flags[:, par, k, :], source).then_inc(flags_in[par], 16)

                def blocks(i):
                    for par in range(2):
                        b = 2 * i + par
                        wait(sp, scans_ready, b + (l * NBLOCKS - 1))
                        load_flags(i, par)

                repeat(sp, NBLOCKS // 2, blocks)
                sp.wait_ge(agg_ready, l + 1)
                sp.dma_start(agg_dram.rearrange("(c p) d -> p c d", p=P), sums[:, :, H:SUMC]).then_inc(agg_stored, 16)
                sp.wait_ge(q_psum, NQUADS * (l + 1))

            typed(0)
            for l in range(L):
                build_table(l)
                attend(l)
                typed(l + 1)
            for par in range(2):
                sp.wait_ge(scattered[par], 64 * HALF_GROUPS * (L + 1))

        @block.gpsimd
        def _(pool):
            chain = Chain(pool, pool_chain)

            nc.gpsimd.iota(iota_i, [[1, P]], channel_multiplier=0).then_inc(pool_const, 1)
            nc.gpsimd.iota(part_i, [[0, 1]], channel_multiplier=1).then_inc(pool_const, 1)
            nc.gpsimd.iota(slot_i, [[P, SCOLS]], channel_multiplier=1).then_inc(pool_const, 1)
            nc.gpsimd.iota(node_i, [[1, NTILES]], channel_multiplier=NTILES).then_inc(pool_const, 1)
            pool.wait_ge(place_ready, 1)
            pool.wait_ge(place_init, 16)
            pool.wait_ge(pool_const, 4)
            for c in range(NTILES):
                pool.indirect_dma_start(out=node_of_place, out_offset=bass.IndirectOffsetOnAxis(ap=place_i[:, c:c + 1], axis=0),
                                        in_=node_i[:, c:c + 1], in_offset=None,
                                        bounds_check=P * SORTED_TILES - 1, oob_is_err=False).then_inc(place_done, 16)
            pool.wait_ge(slot_rows_ready, 1)
            pool.wait_ge(rows_built, 64)
            for c in range(SCOLS):
                pool.indirect_dma_start(out=srow[:, c].rearrange("p k e -> p (k e)"), out_offset=None, in_=edge_rows,
                                        in_offset=bass.IndirectOffsetOnAxis(ap=slot_et_i[:, c:c + 1], axis=0)).then_inc(slot_rows_in, 16)
            pool.wait_ge(prep_done, 1)

            def typed(ph):
                if ph > 0:
                    pool.wait_ge(agg_stored, 16 * ph)

                def gather(i, par):
                    g = 2 * i + par
                    into = g_in if ph > 0 else g_hn
                    if ph == 0:
                        wait(pool, hnT_psum, g - 1)
                        wait(pool, stored[par], i * 16)
                    else:
                        wait(pool, inT_psum, g + ((ph - 1) * GROUPS - 1))
                    for t in range(GROUP):
                        pool.indirect_dma_start(out=into[:, par, t], out_offset=None, in_=x if ph == 0 else agg_dram,
                                                in_offset=bass.IndirectOffsetOnAxis(ap=gather_node[:, g * GROUP + t:g * GROUP + t + 1], axis=0)
                                                ).then_inc(gathered[par], 16)

                def power(g, ready, done):
                    pool.wait_ge(ready, g + 1)
                    nc.gpsimd.tensor_tensor(rstd[:, g % 2], var_eps[:, g % 2], minus_half[:, :], ALU.pow).then_inc(done, 1)

                def scatter(g):
                    pool.wait_ge(out_ready, g + (ph * GROUPS + 1))
                    for t in range(GROUP):
                        source = g_out[:, g % 2, t] if ph < 2 else g_out[:, g % 2, t, 0:D]
                        n = g * GROUP + t
                        pool.indirect_dma_start(out=qkv_dram if ph < 2 else out,
                                                out_offset=bass.IndirectOffsetOnAxis(ap=scatter_node[:, n:n + 1], axis=0),
                                                in_=source, in_offset=None, bounds_check=N - 1, oob_is_err=False
                                                ).then_inc(scattered[g % 2], 16)

                gather(0, 0)
                gather(0, 1)
                if ph > 0:
                    power(GROUPS * (ph - 1), var_ready, rstd_ready)
                for g in range(GROUPS):
                    if g + 2 < GROUPS:
                        gather(g // 2 + 1, g % 2)
                    if ph > 0 and g + 1 < GROUPS:
                        power(GROUPS * (ph - 1) + g + 1, var_ready, rstd_ready)
                    if ph == 2:
                        power(g, var2_ready, rstd2_ready)
                    scatter(g)

            def build_table(l):
                def tile(i, k):
                    c = 4 * i + k
                    par = k % 2
                    pool.wait_ge(kvq_in[k], 16 * i + 16 * kvq_uses(l, 0, k) + 16)
                    wait(pool, spread_T, 2 * c + (2 * l * NTILES - 2))
                    kv = kvq[:, k, D:3 * D].rearrange("p (k d) -> p k d", d=HS)
                    r1 = resid1[:, D:3 * D].rearrange("p (k d) -> p k d", d=HS)
                    r2 = resid2[:, D:3 * D].rearrange("p (k d) -> p k d", d=HS)
                    pool.sem_inc(passed, 1)
                    chain.step(nc.gpsimd.tensor_copy(x_spread[:, par, :, 0:3, :], bc(kv, 2, 3)))
                    chain.wait()
                    chain.step(nc.gpsimd.tensor_tensor(r1, kv, x_spread[:, par, :, 0, :], ALU.subtract))
                    chain.wait()
                    pool.sem_inc(passed, 1)
                    chain.step(nc.gpsimd.tensor_copy(x_spread[:, par, :, 3:6, :], bc(r1, 2, 3)))
                    chain.wait()
                    chain.step(nc.gpsimd.tensor_tensor(r2, r1, x_spread[:, par, :, 3, :], ALU.subtract))
                    chain.wait()
                    pool.sem_inc(passed, 1)
                    nc.gpsimd.tensor_copy(x_spread[:, par, :, 6:8, :], bc(r2, 2, 2)).then_inc(spread_ready, 1)

                def four(i):
                    for k in range(4):
                        tile(i, k)

                repeat(pool, FOURS, four, chain)
                tile(FOURS, 0)

            def attend(l):
                for par in range(2):
                    pool.wait_ge(table_stored[par], 16 * stage_uses(l + 1, 0, par))

                def gather(b, par, q):
                    quad = b * QPB + (l * NQUADS + q)
                    wait(pool, prod_ready, quad - (QPB - 1))
                    if not (isinstance(b, int) and b < 2):
                        pool.wait_ge(sum_psum, 2 * quad - 30)
                    if q == 0:
                        pool.wait_ge(keys_ready, b + (l * NBLOCKS + 1))
                    pool.sem_inc(passed, 1)
                    for s in range(QUAD):
                        pool.indirect_dma_start(out=rows[:, par, q * QUAD + s], out_offset=None, in_=table,
                                                in_offset=bass.IndirectOffsetOnAxis(ap=block_keys[:, par, q * QUAD + s:q * QUAD + s + 1], axis=0)
                                                ).then_inc(rows_in[q], 16)

                for b in range(2):
                    for q in range(QPB):
                        gather(b, b, q)
                with pool.Fori(1, NBLOCKS // 2) as i:
                    for par in range(2):
                        for q in range(QPB):
                            gather(2 * i + par, par, q)

            typed(0)
            for l in range(L):
                build_table(l)
                attend(l)
                typed(l + 1)

        @block.scalar
        def _(act):
            chain = Chain(act, act_chain)

            for l in range(L):
                for k, w in enumerate((Watt, Wmsg)):
                    for h in range(H):
                        act.dma_start(rel_f[h * HS:(h + 1) * HS, l, k * RT * HS:(k + 1) * RT * HS].rearrange("d (t o) -> d t o", o=HS),
                                      w[l, h].rearrange("t d o -> d t o")).then_inc(rel_in, 16)
                for h in range(H):
                    act.dma_start(rel_pri[h * HS:(h + 1) * HS, l, :], pri[l, h:h + 1, :].to_broadcast([HS, RT])).then_inc(rel_in, 16)

            def typed(ph):
                by_tile = lambda b_: b_[:, :].rearrange("p (t d) -> p t d", t=GROUP)
                if ph > 0:
                    act.wait_ge(layer_const_in, 64 * ph)
                    nc.scalar.activation(alpha_t[:, :], alpha_t[:, :], ACT.Exp, scale=-1.0).then_inc(alpha_exp, 1)

                def project(i, par):
                    g = 2 * i + par
                    act.wait_ge(inT_psum, g + ((ph - 1) * GROUPS + 1))
                    wait(act, z_psum, g + ((ph - 1) * GROUPS - 1))
                    nc.scalar.copy(g_inT[:, par], by_tile(bank[0])).then_inc(inT_ready, 1)
                    act.wait_ge(z_psum, g + ((ph - 1) * GROUPS + 1))
                    nc.scalar.activation(g_th[:, par], by_tile(bank[1]), ACT.Tanh, scale=0.5).then_inc(tanh_done, 1)

                def produce(i, par):
                    g = 2 * i + par
                    act.wait_ge(hnT_psum, g + (ph * GROUPS + 1))
                    wait(act, out_psum, g + (ph * GROUPS - 1))
                    nc.scalar.copy(g_hnT[:, par], by_tile(bank[2])).then_inc(hnT_ready, 1)
                    if ph < 2:
                        act.wait_ge(out_psum, g + (ph * GROUPS + 1))
                        wait(act, scattered[par], 64 * i + 64 * ph * HALF_GROUPS)
                        for t in range(GROUP):
                            ins = nc.scalar.copy(g_out[:, par, t], bank[3 + t][:, 0:3 * D])
                        ins.then_inc(out_ready, 1)

                def groups(i):
                    if ph > 0:
                        project(i, 1)
                    produce(i, 0)
                    if ph > 0 and not (isinstance(i, int) and i == HALF_GROUPS - 1):
                        project(i + 1, 0)
                    produce(i, 1)

                if ph > 0:
                    project(0, 0)
                repeat(act, HALF_GROUPS - 1, groups)
                groups(HALF_GROUPS - 1)

            def build_table(l):
                def tile(i, k):
                    c = 4 * i + k
                    par = k % 2
                    for half in range(2):
                        act.wait_ge(spread_T, 2 * c + (2 * l * NTILES + half + 1))
                        wait(act, table_psum, 16 * c + (16 * l * NTILES - 16))
                        nc.scalar.copy(x_spreadT[:, par, half * H:(half + 1) * H, :],
                                       bank[half][:, :].bitcast(BF16).rearrange("p (k n) -> p k n", k=H)).then_inc(spreadT_ready, 1)
                    wait(act, table_stored[par], 32 * i + 16 * stage_uses(l, 0, k))
                    for n in range(0, 2 * H, 2):
                        act.wait_ge(table_psum, 16 * c + (16 * l * NTILES + n + 1))
                        nc.scalar.copy(stage[:, par, :, n * HS:(n + 1) * HS],
                                       bank[2 + n % 6][:, :].rearrange("p (t o) -> p t o", t=RT)).then_inc(stage_act, 1)

                def four(i):
                    for k in range(4):
                        tile(i, k)

                repeat(act, FOURS, four)
                tile(FOURS, 0)

            def attend(l):
                def keys(b, par):
                    nc.scalar.copy(block_keys[:, par, :], key_of[:, bass.ds(b * BLOCK, BLOCK)]).then_inc(keys_ready, 1)

                def mark(b, par, q):
                    quad = b * QPB + (l * NQUADS + q)
                    if not (isinstance(b, int) and b < 2):
                        act.wait_ge(sum_psum, 2 * quad - 30)
                    for s in range(QUAD):
                        chain.step(nc.scalar.activation(onehots[:, par, q * QUAD + s], iota_free[:, :], ACT.Abs,
                                                        bias=minus_dst[:, bass.ds(b * BLOCK + (q * QUAD + s), 1)]))
                    chain.wait()
                    nc.scalar.activation(onehots[:, par, q * QUAD:(q + 1) * QUAD], onehots[:, par, q * QUAD:(q + 1) * QUAD], ACT.Relu,
                                         scale=-1.0, bias=1.0).then_inc(onehot_ready, 1)

                def mark_ahead(b, par, q):
                    if q + 3 < QPB:
                        mark(b, par, q + 3)
                    elif is_block(b + 1):
                        mark(b + 1, 1 - par, q + 3 - QPB)

                def turned(b, par, q):
                    quad = b * QPB + (l * NQUADS + q)
                    act.wait_ge(onehotT_psum, quad + 1)
                    wait(act, q_psum, quad - 1)
                    nc.scalar.copy(onehotT[:, q % 2], bank[0][:, :].rearrange("p (s e) -> p s e", s=QUAD)).then_inc(onehotT_ready, 1)

                def block_of(b, par):
                    for q in range(QPB):
                        if is_block(b):
                            if q + 2 < QPB:
                                turned(b, par, q + 2)
                            elif is_block(b + 1):
                                turned(b + 1, 1 - par, q + 2 - QPB)
                            if q == 0 and is_block(b + 1):
                                wait(act, prod_ready, b * QPB + l * NQUADS)
                                keys(b + 1, 1 - par)
                        if q == 4 and is_block(b - 1):
                            before = b + (l * NBLOCKS - 1)
                            act.wait_ge(below_ready, before + 1)
                            nc.scalar.activation(rows[:, 1 - par, :, RHS0:D], below_max[:, :, :], ACT.Exp).then_inc(exp_ready, 1)
                            act.wait_ge(lower_ready, before + 1)
                            nc.scalar.activation(lower[:, :], lower[:, :], ACT.Exp).then_inc(exp_ready, 1)
                        if is_block(b):
                            mark_ahead(b, par, q)

                act.wait_ge(prep_done, 1)
                wait(act, prod_ready, l * NQUADS)
                keys(0, 0)
                act.wait_ge(table_psum, 16 * NTILES * (l + 1))
                for q in range(3):
                    mark(0, 0, q)
                for q in range(2):
                    turned(0, 0, q)
                block_of(0, 0)
                start = chain.n
                block_of(1, 1)
                block_of(2, 0)
                per = chain.n - start
                with act.Fori(1, NBLOCKS // 2 - 1) as i:
                    chain.n = i * per + start
                    block_of(2 * i + 1, 1)
                    block_of(2 * i + 2, 0)
                chain.n = start + per * (NBLOCKS // 2 - 1)
                block_of(NBLOCKS - 1, 1)
                block_of(NBLOCKS, 0)

            typed(0)
            for l in range(L):
                build_table(l)
                attend(l)
                typed(l + 1)

        @block.tensor
        def _(pe):
            pe.wait_ge(counted, 1)
            nc.tensor.matmul(bank[0][:, 0:NT], upper, ranks[:, :, NTILES - 1], start=True, stop=True)
            nc.tensor.matmul(bank[1][:, 0:NT], ones[:, :], ranks[:, :, NTILES - 1], start=True, stop=True).then_inc(placed_psum, 1)
            pe.wait_ge(bound_counted, 1)
            nc.tensor.matmul(bank[2][:, 0:NTILES - 1], ones[:, :], bounds, start=True, stop=True).then_inc(bound_psum, 1)
            pe.wait_ge(slot_calc, 1)
            n = 0
            for c in range(SCOLS):
                if c:
                    pe.wait_ge(slot_copied, c)
                nc.tensor.transpose(bank[3][:, 0:P], srow[:, c, 0, :], ident[:, :])
                nc.tensor.transpose(bank[4][:, 0:P], s_loc[:, c, :], ident[:, :])
                nc.tensor.transpose(bank[5][:, 0:P], s_valid[:, c, :], ident[:, :])
                nc.tensor.matmul(bank[6][0:1, 0:P], cross_col[:, c:c + 1], ident[:, :], start=True, stop=True)
                nc.tensor.matmul(bank[7][0:1, 0:P], slot_dt[:, c:c + 1], ident[:, :], start=True, stop=True).then_inc(slot_T, 1)

            def typed(ph):
                pe.wait_ge(weights_in, 16 * (6, 6 + 8, 6 + 8 + 3)[ph])
                if ph == 0:
                    pe.wait_ge(place_loaded, 16)
                    pe.wait_ge(prep_done, 1)

                def tile_types(g):
                    _, types = nc.values_load_multi_w_load_instructions(
                        tile_type[0:1, bass.ds(g * GROUP, GROUP)], engines=[PE_], min_val=0, max_val=NT - 1,
                        skip_runtime_bounds_check_because="a count of comparisons with 15 tile numbers")
                    return types

                def project(i, par):
                    g = 2 * i + par
                    types = tile_types(g)
                    pe.wait_ge(gathered[par], 64 * i + 64 * (ph * HALF_GROUPS + 1))
                    wait(pe, inT_ready, g + (ph - 1) * GROUPS)
                    for t in range(GROUP):
                        ins = nc.tensor.transpose(bank[0][:, t * P:(t + 1) * P], g_in[:, par, t], ident[:, :])
                    ins.then_inc(inT_psum, 1)
                    pe.wait_ge(inT_ready, g + ((ph - 1) * GROUPS + 1))
                    wait(pe, z_used, g + (ph - 1) * GROUPS)
                    for t in range(GROUP):
                        ins = nc.tensor.matmul(bank[1][:, t * D:(t + 1) * D], g_inT[:, par, t],
                                               w_a[:, bass.ds(types[t], 1), :].rearrange("p a n -> p (a n)"), start=True, stop=True)
                    ins.then_inc(z_psum, 1)

                def produce(i, par):
                    g = 2 * i + par
                    if ph < 2:
                        types = tile_types(g)
                    if ph > 0:
                        pe.wait_ge(hn_ready, g + ((ph - 1) * GROUPS + 1))
                    else:
                        pe.wait_ge(gathered[par], 64 * i + 64)
                    wait(pe, hnT_ready, g + ph * GROUPS)
                    for t in range(GROUP):
                        ins = nc.tensor.transpose(bank[2][:, t * P:(t + 1) * P], g_hn[:, par, t], ident[:, :])
                    ins.then_inc(hnT_psum, 1)
                    pe.wait_ge(hnT_ready, g + (ph * GROUPS + 1))
                    wait(pe, out_ready, g + ph * GROUPS)
                    for t in range(GROUP):
                        if ph < 2:
                            ins = nc.tensor.matmul(bank[3 + t][:, 0:3 * D], g_hnT[:, par, t],
                                                   w_qkv[:, bass.ds(types[t], 1), :].rearrange("p a n -> p (a n)"), start=True, stop=True)
                        else:
                            ins = nc.tensor.matmul(bank[3][:, t * D:(t + 1) * D], g_hnT[:, par, t], w_ff, start=True, stop=True)
                    ins.then_inc(out_psum, 1)

                def groups(i):
                    if ph > 0:
                        project(i, 1)
                    produce(i, 0)
                    if ph > 0 and not (isinstance(i, int) and i == HALF_GROUPS - 1):
                        project(i + 1, 0)
                    produce(i, 1)

                if ph > 0:
                    project(0, 0)
                repeat(pe, HALF_GROUPS - 1, groups)
                groups(HALF_GROUPS - 1)

            def build_table(l):
                pe.wait_ge(w_rel_in, 16 * 2 * PARTS * (l + 1))

                def tile(i, j):
                    c = 4 * i + j
                    par = j % 2
                    pe.wait_ge(spread_ready, c + (l * NTILES + 1))
                    for half in range(2):
                        wait(pe, spreadT_ready, 2 * c + (2 * l * NTILES + half - 1))
                        for k in range(H):
                            ins = nc.tensor.transpose(bank[half][:, :].bitcast(BF16)[:, k * P:(k + 1) * P],
                                                      x_spread[:, par, half * H + k].rearrange("p w d -> p (w d)"), identb[:, :])
                        ins.then_inc(spread_T, 1)
                    for k in range(2 * H):
                        if k % H == 0:
                            pe.wait_ge(spreadT_ready, 2 * c + (2 * l * NTILES + k // H + 1))
                        last_use = k - 6 if k >= 6 else k + 12 - 2 * H if k < 4 else k + 6 - 2 * H
                        wait(pe, stage_act if k % 2 == 0 else stage_dve, H * c + (H * l * NTILES + last_use // 2 + 1))
                        nc.tensor.matmul(bank[2 + k % 6][:, :], x_spreadT[:, par, k, :], w_rel[:, k, :], start=True, stop=True).then_inc(table_psum, 1)

                def four(i):
                    for k in range(4):
                        tile(i, k)

                repeat(pe, FOURS, four)
                tile(FOURS, 0)

            def attend(l):
                def slot_tiles(b, q):
                    _, tiles = nc.values_load_multi_w_load_instructions(
                        dst_tile[0:1, bass.ds(b * BLOCK + q * QUAD, 2 * QUAD)], engines=[PE_], min_val=0, max_val=NTILES - 1,
                        skip_runtime_bounds_check_because="a count of comparisons with 48 tile numbers")
                    return tiles

                def turn(b, par, q):
                    quad = b * QPB + (l * NQUADS + q)
                    pe.wait_ge(onehot_ready, quad + 1)
                    wait(pe, onehotT_ready, quad)
                    for s in range(QUAD):
                        ins = nc.tensor.transpose(bank[0][:, s * P:(s + 1) * P], onehots[:, par, q * QUAD + s], ident[:, :])
                    ins.then_inc(onehotT_psum, 1)

                def fetch_q(b, par, q, tiles):
                    quad = b * QPB + (l * NQUADS + q)
                    pe.wait_ge(onehotT_ready, quad + 1)
                    wait(pe, prod_ready, quad - 1)
                    for s in range(QUAD):
                        for k in range(3):
                            ins = nc.tensor.matmul(bank[1 + q % 2][:, s * D:(s + 1) * D], onehotT[:, q % 2, s],
                                                   q_parts[:, bass.ds(tiles[s], 1), k, :].rearrange("p a n -> p (a n)"),
                                                   start=(k == 0), stop=(k == 2))
                    ins.then_inc(q_psum, 1)

                def sum_quad(b, par, q):
                    quad = b * QPB + (l * NQUADS + q)
                    pe.wait_ge(weighted, quad + 1)
                    for pair in range(2):
                        wait(pe, sum_added, 4 * quad + (2 * pair - 2))
                        for s in range(2):
                            slot = q * QUAD + 2 * pair + s
                            ins = nc.tensor.matmul(bank[5 + pair][:, s * SUMC:(s + 1) * SUMC], onehots[:, par, slot],
                                                   rows[:, par, slot, RHS0:TABLE_ROW], start=True, stop=True)
                        ins.then_inc(sum_psum, 1)

                def block_of(b, par):
                    before = b + (l * NBLOCKS - 1)
                    for q in range(QPB):
                        if is_block(b - 1) and q == FIRST_SUMMED:
                            pe.wait_ge(cross_ready, before + 1)
                            nc.tensor.matmul(bank[4][:, 0:H], cross_hot[:, :], lower[:, :], start=True, stop=True).then_inc(rescale_psum, 1)
                        late = late_quad(b, par, q, FIRST_SUMMED)
                        if is_block(late[0]):
                            sum_quad(*late)
                        if is_block(b):
                            if q + 2 < QPB:
                                turn(b, par, q + 2)
                            elif is_block(b + 1):
                                turn(b + 1, 1 - par, q + 2 - QPB)
                            if q % 2 == 0:
                                tiles = slot_tiles(b, q + 1)
                            if q + 1 < QPB:
                                fetch_q(b, par, q + 1, tiles[QUAD * (q % 2):])
                            elif is_block(b + 1):
                                fetch_q(b + 1, 1 - par, 0, tiles[QUAD:])
                        if not is_block(b - 1):
                            continue
                        if q == 0:
                            pe.wait_ge(masked_ready, before + 1)
                            for n in range(PER_CHUNK):
                                ins = nc.tensor.transpose(bank[3][:, n * P:(n + 1) * P],
                                                          masked[:, n].rearrange("p j h -> p (j h)"), ident[:, :])
                            ins.then_inc(masked_T, 1)
                        if q == 1:
                            pe.wait_ge(scans_ready, before + 1)
                            by_head = ident[:, :].rearrange("p (j h) -> p h j", h=H)
                            for n, column in enumerate((fwd[:, CLEN - 1:CLEN], first_seg[:, CLEN - 1:CLEN], bwd[:, 0:1], last_seg[:, 0:1])):
                                ins = nc.tensor.matmul(bank[4][0:1, n * P:(n + 1) * P].rearrange("o (h j) -> o h j", h=H),
                                                       column, by_head, start=True, stop=True)
                            ins.then_inc(chunk_rows, 1)
                        if q == 2:
                            pe.wait_ge(carry_ready, before + 1)
                            for n in range(2):
                                ins = nc.tensor.matmul(bank[4][:, n:n + 1], carry_rows[0:1, n].rearrange("o j h -> o (j h)"),
                                                       ones[0:1, 0:1], start=True, stop=True)
                            ins.then_inc(carry_T, 1)
                        if q == 3:
                            pe.wait_ge(max_ready, before + 1)
                            for n in range(PER_CHUNK):
                                ins = nc.tensor.transpose(bank[3][:, n * P:(n + 1) * P], edge_max[:, n * P:(n + 1) * P], ident[:, :])
                            ins.then_inc(max_T, 1)

                pe.wait_ge(q_split, NTILES * (l + 1))
                turn(0, 0, 0)
                turn(0, 0, 1)
                fetch_q(0, 0, 0, slot_tiles(0, 0))
                block_of(0, 0)
                block_of(1, 1)
                block_of(2, 0)
                with pe.Fori(1, NBLOCKS // 2 - 1) as i:
                    block_of(2 * i + 1, 1)
                    block_of(2 * i + 2, 0)
                block_of(NBLOCKS - 1, 1)
                block_of(NBLOCKS, 0)
                for q in range(FIRST_SUMMED):
                    sum_quad(*late_quad(NBLOCKS + 1, 1, q, FIRST_SUMMED))

            typed(0)
            for l in range(L):
                build_table(l)
                attend(l)
                typed(l + 1)

        @block.vector
        def _(dve):
            v = nc.vector
            chain = Chain(dve, dve_chain)

            def link(instruction):
                chain.step(instruction)
                chain.wait()

            def split_relations(l):
                link(v.tensor_scalar(rel_pri[:, l], rel_pri[:, l], HS ** -0.5, None, ALU.mult))
                att = rel_f[:, l, 0:RT * HS].rearrange("p (t o) -> p t o", o=HS)
                link(v.tensor_tensor(att, att, bc(rel_pri[:, l], 2, HS), ALU.mult))
                both = rel_f[:, l].rearrange("p (k n) -> p k n", k=2)
                left = rel_r.rearrange("p (k n) -> p k n", k=2)
                link(v.tensor_copy(rel_p[:, l, :, 0, :], both))
                link(v.tensor_tensor(left, both, rel_p[:, l, :, 0, :], ALU.subtract))
                link(v.tensor_copy(rel_p[:, l, :, 1, :], left))
                link(v.tensor_tensor(left, left, rel_p[:, l, :, 1, :], ALU.subtract))
                v.tensor_copy(rel_p[:, l, :, 2, :], left).then_inc(rel_split, 1)

            v.memset(nt_i, NT)
            v.memset(src_i, 0)
            v.memset(typ_i, 0)
            v.memset(dst_i, int(NO_DST))
            v.memset(no_node, int(NO_NODE))
            v.memset(zeros, 0.0)
            v.memset(pad_dst, NO_DST)
            v.memset(pad_key, 0.0)
            v.memset(before_first, -1.0).then_inc(pads_set, 1)
            v.memset(ones[:, :], 1.0)
            v.memset(minus_half[:, :], -0.5)
            v.memset(keep, 1.0)
            v.memset(carry_in[0:1, :, :, :, :], -BIG)
            dve.wait_ge(pool_const, 4)
            v.tensor_copy(iota_free[:, :], iota_i)
            link(v.tensor_copy(part_f, part_i))
            v.memset(keep[:, :, 0:1], 0.0)
            v.tensor_scalar(identb[:, :], iota_free[:, :], part_f, None, ALU.is_equal)
            v.tensor_scalar(upper, iota_free[:, :], part_f, None, ALU.is_gt)
            link(v.tensor_scalar(ident[:, :], iota_free[:, :], part_f, None, ALU.is_equal))

            dve.wait_ge(type_in, 32)
            v.tensor_copy(type_no[:, :], iota_free[:, 0:NT])
            link(v.tensor_copy(nt_f, nt_i))
            link(v.tensor_tensor(onehot_t, bc(nt_f, 1, NT), bc(type_no[:, :], 2, NTILES), ALU.is_equal))
            flat = lambda ap: ap.rearrange("p t c -> p (t c)")
            v.tensor_tensor_scan(flat(ranks), flat(keep), flat(onehot_t), 0.0, ALU.mult, ALU.add).then_inc(counted, 1)
            dve.wait_ge(placed_psum, 1)
            link(v.tensor_scalar(tot, bank[1][:, 0:NT], 127.0, None, ALU.add))
            link(v.tensor_copy(tot_i, tot))
            link(v.tensor_single_scalar(tot_i, tot_i, 7, ALU.logical_shift_right))
            link(v.tensor_copy(tiles_t, tot_i))
            link(v.tensor_tensor_scan(first_tile, ones[:, 0:NT], tiles_t, 0.0, ALU.mult, ALU.add))
            link(v.tensor_tensor(first_tile, first_tile, tiles_t, ALU.subtract))
            link(v.scalar_tensor_tensor(base_t, first_tile, float(P), bank[0][:, 0:NT], ALU.mult, ALU.add))
            link(v.tensor_tensor(ranks, ranks, bc(base_t, 2, NTILES), ALU.add))
            link(v.tensor_tensor(ranks, ranks, onehot_t, ALU.mult))
            v.tensor_reduce(is_pad, onehot_t.rearrange("p t c -> p c t"), AX.X, ALU.add)
            link(v.tensor_reduce(pos, ranks.rearrange("p t c -> p c t"), AX.X, ALU.add))
            link(v.tensor_scalar(pos, pos, -1.0, 0.0, ALU.add, ALU.max))
            link(v.tensor_copy(pos_i, pos))
            v.tensor_single_scalar(pos_lo, pos_i, P - 1, ALU.bitwise_and)
            link(v.tensor_single_scalar(pos_hi, pos_i, 7, ALU.logical_shift_right))
            v.tensor_copy(pos_lof, pos_lo)
            link(v.tensor_copy(pos, pos_hi))
            link(v.scalar_tensor_tensor(pos, pos_lof, float(SORTED_TILES), pos, ALU.mult, ALU.add))
            link(v.tensor_scalar(is_pad, is_pad, -100000.0, 100000.0, ALU.mult, ALU.add))
            link(v.tensor_tensor(pos, pos, is_pad, ALU.add))
            v.tensor_copy(place_i, pos).then_inc(place_ready, 1)
            v.tensor_copy(tile_no, iota_free[:, 0:SORTED_TILES])
            link(v.memset(junk[:, 0:1], 0.0))
            link(v.tensor_tensor(type_cmp, bc(tile_no, 2, NT), bc(first_tile, 1, SORTED_TILES), ALU.is_ge))
            link(v.tensor_reduce(type_f, type_cmp, AX.X, ALU.add))
            link(v.tensor_scalar(type_of_tile[:, :], type_f, -1.0, None, ALU.add))
            link(v.tensor_copy(tile_type[:, :], type_of_tile[0:1, :]))

            dve.wait_ge(edge_in, 96)
            v.scalar_tensor_tensor(key_f, src_i, float(RT), typ_i, ALU.mult, ALU.add)
            link(v.tensor_copy(dst_f, dst_i))
            link(v.memset(junk[:, 0:1], 0.0))
            v.memset(pad_lo, 0.0).then_inc(flat_ready, 1)
            for d in range(NTILES - 1):
                if d >= 2:
                    chain.wait(chain.n - 1)
                chain.step(v.tensor_scalar((junk, junk_b)[d % 2], dst_f, float(P * (d + 1)), None, ALU.is_lt, ALU.add,
                                           accum_out=bounds[:, d:d + 1]))
            chain.wait()
            v.memset(pad_lo, 0.0).then_inc(bound_counted, 1)
            dve.wait_ge(rel_in, 16 * 3 * H * L)
            for l in range(L):
                if l:
                    dve.wait_ge(rel_split, l)
                split_relations(l)
            dve.wait_ge(bound_psum, 1)
            link(v.tensor_copy(starts_i, bank[2][:, 0:NTILES - 1]))
            link(v.tensor_single_scalar(starts_i, starts_i, 7, ALU.logical_shift_right))
            link(v.tensor_copy(starts, starts_i))
            link(v.scalar_tensor_tensor(starts, starts, 1.0, iota_free[:, 0:NTILES - 1], ALU.add, ALU.add))
            link(v.tensor_copy(slot_no, slot_i))
            link(v.tensor_tensor(slot_cmp, bc(slot_no, 2, NTILES - 1), bc(starts, 1, SCOLS), ALU.is_ge))
            link(v.tensor_reduce(slot_dt, slot_cmp, AX.X, ALU.add))
            link(v.tensor_tensor(slot_et, slot_no, slot_dt, ALU.subtract))
            link(v.tensor_scalar(slot_et, slot_et, float(EROWS - 1), None, ALU.min))
            v.tensor_scalar(slot_base, slot_dt, float(P), None, ALU.mult)
            v.tensor_copy(slot_et_i, slot_et).then_inc(slot_rows_ready, 1)
            dve.wait_ge(slot_rows_in, 16 * SCOLS)
            link(v.tensor_tensor(s_loc, srow[:, :, 1, :], bc(slot_base, 2, P), ALU.subtract))
            link(v.tensor_scalar(s_a, s_loc, 0.0, None, ALU.is_ge))
            link(v.tensor_scalar(s_valid, s_loc, float(P - 1), None, ALU.is_le))
            link(v.tensor_tensor(s_valid, s_valid, s_a, ALU.mult))
            for k in range(2):
                link(v.tensor_tensor(s_a, srow[:, :, 1, :], srow[:, :, 2 + k, :], ALU.not_equal))
                link(v.tensor_tensor(s_flag[:, k], s_a, s_valid, ALU.mult))
            link(v.tensor_tensor(cross_col, s_valid[:, :, 0], s_flag[:, 0, :, 0], ALU.subtract))
            link(v.scalar_tensor_tensor(slot_no, s_loc[:, :, 0], 1.0, cross_col, ALU.add, ALU.mult))
            link(v.tensor_scalar(cross_col, slot_no, -1.0, None, ALU.add))
            link(v.tensor_scalar(s_flag, s_flag, -BIG, None, ALU.mult))
            v.tensor_scalar(s_valid, s_valid, BIG, -BIG, ALU.mult, ALU.add).then_inc(slot_calc, 1)
            for c in range(SCOLS):
                cols = slice(c * P, (c + 1) * P)
                dve.wait_ge(slot_T, c + 1)
                v.tensor_copy(key_of[:, cols], bank[3][:, 0:P])
                v.tensor_scalar(minus_dst[:, cols], bank[4][:, 0:P], -1.0, None, ALU.mult)
                v.tensor_copy(invalid[:, cols], bank[5][:, 0:P])
                v.tensor_copy(crossing[:, c * (P // BLOCK):(c + 1) * (P // BLOCK)],
                              bank[6][0:1, 0:P].rearrange("o (b s) -> o b s", s=BLOCK)[:, :, 0])
                v.tensor_copy(dst_tile[:, cols], bank[7][0:1, 0:P]).then_inc(slot_copied, 1)
            dve.wait_ge(place_loaded, 16)
            link(v.tensor_copy(node_f, scatter_node[:, :]))
            link(v.tensor_scalar(node_f, node_f, float(N - 1), None, ALU.min))
            link(v.tensor_copy(gather_node[:, :], node_f))
            dve.wait_ge(slot_copied, SCOLS)
            dve.wait_ge(flags_stored, 32)
            v.memset(junk[:, 0:1], 0.0).then_inc(prep_done, 1)

            def layer_constants(l):
                dve.wait_ge(alpha_exp, l + 1)
                link(v.tensor_scalar(alpha_t[:, :], alpha_t[:, :], 1.0, None, ALU.add))
                v.tensor_tensor(tile_is_type, bc(type_of_tile[:, :], 2, NT), bc(type_no[:, :], 1, SORTED_TILES), ALU.is_equal)
                link(v.reciprocal(alpha_t[:, :], alpha_t[:, :]))
                link(v.tensor_tensor(tile_is_type, tile_is_type, bc(alpha_t[:, :], 1, SORTED_TILES), ALU.mult))
                link(v.tensor_reduce(half_alpha[:, :], tile_is_type, AX.X, ALU.add))
                link(v.tensor_scalar(one_less_alpha[:, :], half_alpha[:, :], -1.0, 1.0, ALU.mult, ALU.add))
                link(v.tensor_scalar(half_alpha[:, :], half_alpha[:, :], 0.5, None, ALU.mult))
                v.memset(junk2[:, :], 0.0).then_inc(layer_const_ready, 1)

            def statistics(par, rows_, ready):
                for t in range(GROUP):
                    chain.step(v.bn_stats(bn_in[:, par, t, :], rows_[:, t]))
                chain.wait()
                dve.sem_inc(passed, 1)
                for t in range(GROUP):
                    chain.step(v.bn_aggr(mean_var[:, par, t, :], bn_in[:, par, t, :]))
                chain.wait()
                v.tensor_scalar(var_eps[:, par], mean_var[:, par, :, 1], EPS, None, ALU.add).then_inc(ready, 1)

            def typed(ph):
                if ph > 0:
                    layer_constants(ph - 1)

                def combine(i, par):
                    g = 2 * i + par
                    z = bank[1][:, :].rearrange("p (t d) -> p t d", t=GROUP)
                    hh, res, hn = g_h[:, par], g_res[:, par], g_hn[:, par]
                    dve.wait_ge(res_in[par], 16 * ph * i + (16, 16, 16 * HALF_GROUPS + 32)[ph])
                    chain.step(v.tensor_tensor(res, res, bc(one_less_alpha[:, bass.ds(g * GROUP, GROUP)], 2, D), ALU.mult))
                    dve.wait_ge(tanh_done, g + ((ph - 1) * GROUPS + 1))
                    v.scalar_tensor_tensor(hh, g_th[:, par], 1.0, z, ALU.add, ALU.mult).then_inc(z_used, 1)
                    dve.wait_ge(z_used, g + ((ph - 1) * GROUPS + 1))
                    for t in range(GROUP):
                        chain.step(v.scalar_tensor_tensor(hh[:, t], hh[:, t], half_alpha[:, bass.ds(g * GROUP + t, 1)], res[:, t],
                                                          ALU.mult, ALU.add))
                    chain.wait()
                    statistics(par, hh, var_ready)
                    dve.wait_ge(rstd_ready, g + ((ph - 1) * GROUPS + 1))
                    for t in range(GROUP):
                        chain.step(v.tensor_scalar(hh[:, t], hh[:, t], mean_var[:, par, t, 0:1], rstd[:, par, t:t + 1],
                                                   ALU.subtract, ALU.mult))
                    chain.wait()
                    link(v.tensor_tensor(hh, hh, bc(row_const[:, 0, :], 1, GROUP), ALU.mult))
                    wait(dve, hnT_psum, g + (ph * GROUPS - 1))
                    wait(dve, stored[par], 16 * i + 16 * HALF_GROUPS if ph == 1 else 32 * HALF_GROUPS)
                    v.tensor_tensor(hn, hh, bc(row_const[:, 1, :], 1, GROUP), ALU.add).then_inc(hn_ready, 1)

                def finish(i, par):
                    g = 2 * i + par
                    dve.wait_ge(out_psum, g + (2 * GROUPS + 1))
                    y = g_h[:, par]
                    link(v.tensor_tensor(y, bank[3][:, :].rearrange("p (t d) -> p t d", t=GROUP), bc(row_const[:, 2, :], 1, GROUP), ALU.add))
                    link(v.tensor_tensor(y, y, g_x[:, par], ALU.add))
                    statistics(par, y, var2_ready)
                    dve.wait_ge(rstd2_ready, g + 1)
                    wait(dve, scattered[par], 64 * i + 64 * 2 * HALF_GROUPS)
                    for t in range(GROUP):
                        ins = v.tensor_scalar(g_out[:, par, t, 0:D], y[:, t], mean_var[:, par, t, 0:1], rstd[:, par, t:t + 1],
                                              ALU.subtract, ALU.mult)
                    ins.then_inc(out_ready, 1)

                def groups(i):
                    combine(i, 1)
                    if ph == 2:
                        finish(i, 0)
                    if not (isinstance(i, int) and i == HALF_GROUPS - 1):
                        combine(i + 1, 0)
                    if ph == 2:
                        finish(i, 1)

                if ph > 0:
                    combine(0, 0)
                    repeat(dve, HALF_GROUPS - 1, groups, chain)
                    groups(HALF_GROUPS - 1)

            def build_table(l):
                def tile(i, k):
                    c = 4 * i + k
                    par = k % 2
                    q0, q1, q2 = kvq[:, k, 0:D], resid1[:, 0:D], resid2[:, 0:D]
                    qp = [q_parts[:, bass.ds(c, 1), n, :].rearrange("p c d -> p (c d)") for n in range(3)]
                    dve.wait_ge(kvq_in[k], 16 * i + 16 * kvq_uses(l, 0, k) + 16)
                    link(v.tensor_copy(qp[0], q0))
                    link(v.tensor_tensor(q1, q0, qp[0], ALU.subtract))
                    link(v.tensor_copy(qp[1], q1))
                    link(v.tensor_tensor(q2, q1, qp[1], ALU.subtract))
                    v.tensor_copy(qp[2], q2).then_inc(q_split, 1)
                    wait(dve, table_stored[par], 32 * i + 16 * stage_uses(l, 0, k))
                    for n in range(1, 2 * H, 2):
                        dve.wait_ge(table_psum, 16 * c + (16 * l * NTILES + n + 1))
                        v.tensor_copy(stage[:, par, :, n * HS:(n + 1) * HS],
                                      bank[2 + n % 6][:, :].rearrange("p (t o) -> p t o", t=RT)).then_inc(stage_dve, 1)

                def four(i):
                    for k in range(4):
                        tile(i, k)

                repeat(dve, FOURS, four, chain)
                tile(FOURS, 0)

            def attend(l):
                def multiply(b, par, q):
                    quad = b * QPB + (l * NQUADS + q)
                    dve.wait_ge(rows_in[q], 64 * b + 64 * (l * NBLOCKS + 1))
                    dve.wait_ge(q_psum, quad + 1)
                    v.tensor_tensor(prod[:, q % 2], bank[1 + q % 2][:, :].rearrange("p (s d) -> p s d", s=QUAD),
                                    rows[:, par, q * QUAD:(q + 1) * QUAD, 0:D], ALU.mult).then_inc(prod_ready, 1)

                def head_sums(b, par, q):
                    quad = b * QPB + (l * NQUADS + q)
                    dve.wait_ge(prod_ready, quad + 1)
                    v.tensor_reduce(score[:, par, q * QUAD:(q + 1) * QUAD, :], prod[:, q % 2].rearrange("p s (h o) -> p s h o", h=H),
                                    AX.X, ALU.add).then_inc(score_ready, 1)

                def weigh(b, par, q):
                    part = rows[:, par, q * QUAD:(q + 1) * QUAD, :]
                    msg = part[:, :, D:2 * D].rearrange("p s (h o) -> p s h o", h=H)
                    dve.wait_ge(exp_ready, 2 * b + (2 * l * NBLOCKS + 1))
                    v.tensor_tensor(msg, msg, bc(part[:, :, RHS0:D], 3, HS), ALU.mult).then_inc(weighted, 1)

                def slot_tiles(b, q):
                    _, tiles = nc.values_load_multi_w_load_instructions(
                        dst_tile[0:1, bass.ds(b * BLOCK + q * QUAD, QUAD)], engines=[DVE_], min_val=0,
                        max_val=NTILES - 1, skip_runtime_bounds_check_because="a count of comparisons with 48 tile numbers")
                    return tiles

                def add(b, q, n, tiles):
                    quad = b * QPB + (l * NQUADS + q)
                    dve.wait_ge(sum_psum, 2 * quad + (n // 2 + 1))
                    wait(dve, sum_added, 4 * quad + n)
                    total = sums[:, bass.ds(tiles[n], 1), :].rearrange("p a n -> p (a n)")
                    v.tensor_tensor(total, total, bank[5 + n // 2][:, (n % 2) * SUMC:(n % 2 + 1) * SUMC],
                                    ALU.add).then_inc(sum_added, 1)

                def scale_crossing(b, tiles):
                    dve.wait_ge(rescale_psum, b + (l * NBLOCKS + 1))
                    link(v.tensor_scalar(rescale[:, :], bank[4][:, 0:H], 1.0, None, ALU.add))
                    wait(dve, sum_added, b * BLOCK + l * NQUADS * QUAD)
                    total = sums[:, bass.ds(tiles[0], 1), :].rearrange("p a n -> p (a n)")
                    chain.step(v.tensor_tensor(total[:, 0:H], total[:, 0:H], rescale[:, :], ALU.mult))
                    messages = total[:, H:SUMC].rearrange("p (h o) -> p h o", h=H)
                    link(v.tensor_tensor(messages, messages, bc(rescale[:, :], 2, HS), ALU.mult))

                def find_maxima(b, old, half, q, place):
                    before = b + (l * NBLOCKS - 1)
                    if (q, place) == (0, 0):
                        dve.wait_ge(score_ready, b * QPB + l * NQUADS)
                        v.tensor_tensor(masked[:, :].rearrange("p i j h -> p j i h"), score[:, old].rearrange("p (j i) h -> p j i h", i=PER_CHUNK),
                                        bc(invalid[:, bass.ds(b * BLOCK - BLOCK, BLOCK)].rearrange("p (j i) -> p j i", i=PER_CHUNK), 3, H),
                                        ALU.add).then_inc(masked_ready, 1)
                    if (q, place) == (0, 1):
                        dve.wait_ge(flags_in[old], half * 32 + 32 * (l * NBLOCKS // 2 + 1))
                        chain.step(v.tensor_tensor_scan(first_seg[:, :], flags[:, old, 0, :], flags[:, old, 0, :], 0.0, ALU.min, ALU.min))
                    if (q, place) == (0, 3):
                        chain.step(v.tensor_tensor_scan(last_seg[:, ::-1], flags[:, old, 1, ::-1], flags[:, old, 1, ::-1], 0.0, ALU.min, ALU.min))
                    if (q, place) == (1, 0):
                        dve.wait_ge(masked_T, before + 1)
                        chain.step(v.tensor_tensor_scan(fwd[:, :], flags[:, old, 0, :], bank[3][:, 0:CLEN], -BIG, ALU.add, ALU.max))
                    if (q, place) == (1, 1):
                        chain.wait()
                        v.tensor_tensor_scan(bwd[:, ::-1], flags[:, old, 1, ::-1], fwd[:, ::-1], -BIG, ALU.add, ALU.max).then_inc(scans_ready, 1)
                    if (q, place) == (2, 0):
                        dve.wait_ge(chunk_rows, before + 1)
                        got = bank[4][0:1, :].rearrange("o (k h j) -> o k h j", k=4, h=H)
                        for n in range(2):
                            at = 1 - n
                            chain.step(v.tensor_copy(carry_in[0:1, n, :, :, at:at + CHUNKS], got[:, 2 * n:2 * n + 2]))
                        chain.step(v.tensor_copy(carry_in[0:1, 0, 0, :, 0], carried[:, :]))
                    if (q, place) == (2, 1):
                        row = lambda ap: ap.rearrange("o h j -> o (h j)")
                        chain.wait()
                        chain.step(v.tensor_tensor_scan(row(carry_out[0:1, 0]), row(carry_in[0:1, 0, 1]), row(carry_in[0:1, 0, 0]),
                                                        -BIG, ALU.add, ALU.max))
                        chain.step(v.tensor_tensor_scan(row(carry_out[0:1, 1])[:, ::-1], row(carry_in[0:1, 1, 1])[:, ::-1],
                                                        row(carry_in[0:1, 1, 0])[:, ::-1], -BIG, ALU.add, ALU.max))
                    if (q, place) == (2, 2):
                        chain.wait()
                        chain.step(v.tensor_copy(carry_rows[0:1, 0], carry_out[0:1, 0, :, 0:CHUNKS].rearrange("o h j -> o j h")))
                        v.tensor_copy(carry_rows[0:1, 1], carry_out[0:1, 1, :, 1:CHUNKS + 1].rearrange("o h j -> o j h")
                                      ).then_inc(carry_ready, 1)
                    if (q, place) == (3, 0):
                        dve.wait_ge(carry_T, before + 1)
                        chain.step(v.tensor_copy(chunk_carry[:, :], bank[4][:, 0:2]))
                    if (q, place) == (3, 1):
                        chain.wait()
                        chain.step(v.scalar_tensor_tensor(edge_max[:, :], first_seg[:, :], chunk_carry[:, 0:1], bwd[:, :], ALU.add, ALU.max))
                    if (q, place) == (3, 2):
                        chain.wait()
                        v.scalar_tensor_tensor(edge_max[:, :], last_seg[:, :], chunk_carry[:, 1:2], edge_max[:, :], ALU.add,
                                               ALU.max).then_inc(max_ready, 1)
                    if (q, place) == (4, 0):
                        dve.wait_ge(max_T, before + 1)
                        by_half = lambda ap: ap.rearrange("p (j i) h -> p i j h", i=PER_CHUNK)
                        v.tensor_tensor(by_half(below_max[:, :, :]), masked[:, :],
                                        bank[3][:, 0:CLEN].rearrange("p (i j h) -> p i j h", i=PER_CHUNK, h=H),
                                        ALU.subtract).then_inc(below_ready, 1)
                        chain.step(v.tensor_tensor(lower[:, :], carry_in[0:1, 0, 0, :, 0], bank[3][0:1, 0:H], ALU.subtract))
                        v.tensor_copy(carried[:, :], carry_out[0:1, 0, :, CHUNKS])
                        v.tensor_scalar(cross_hot[:, :], iota_free[0:1, :], crossing[:, bass.ds(b - 1, 1)], None, ALU.is_equal)
                    if (q, place) == (4, 1):
                        chain.wait()
                        v.tensor_scalar(lower[:, :], lower[:, :], 0.0, None, ALU.min).then_inc(lower_ready, 1)
                    if (q, place) == (4, 3):
                        dve.wait_ge(exp_ready, 2 * before + 2)
                        v.tensor_scalar(lower[:, :], lower[:, :], -1.0, None, ALU.add).then_inc(cross_ready, 1)

                def step(b, par, half, q):
                    late, weigh_next = late_quad(b, par, q, FIRST_SUMMED), late_quad(b, par, q, FIRST_WEIGHED)
                    adding, maxima = is_block(late[0]), is_block(b - 1)
                    if adding:
                        tiles = slot_tiles(late[0], late[2])
                    if is_block(b):
                        multiply(b, par, q)
                    if adding and q == FIRST_SUMMED:
                        scale_crossing(b - 1, tiles)
                    for place in range(4):
                        if adding:
                            add(late[0], late[2], place, tiles)
                        if place == 1 and is_block(b):
                            head_sums(b, par, q)
                        if place == 3 and is_block(weigh_next[0]):
                            weigh(*weigh_next)
                        if maxima:
                            find_maxima(b, 1 - par, half, q, place)

                def block_of(b, par, half):
                    for q in range(QPB):
                        step(b, par, half, q)

                v.memset(carried[:, :], -BIG)
                dve.wait_ge(spread_ready, NTILES * (l + 1))
                if l:
                    dve.wait_ge(agg_stored, 16 * l)
                link(v.memset(sums[:, :, :], 0.0))
                block_of(0, 0, None)
                chain_start = chain.n
                block_of(1, 1, 0)
                block_of(2, 0, 0)
                per = chain.n - chain_start
                with dve.Fori(1, NBLOCKS // 2 - 1) as i:
                    chain.n = i * per + chain_start
                    block_of(2 * i + 1, 1, i)
                    block_of(2 * i + 2, 0, i)
                chain.n = chain_start + per * (NBLOCKS // 2 - 1)
                block_of(NBLOCKS - 1, 1, NBLOCKS // 2 - 1)
                block_of(NBLOCKS, 0, NBLOCKS // 2 - 1)
                for q in range(FIRST_SUMMED):
                    step(NBLOCKS + 1, 1, None, q)
                dve.wait_ge(sum_added, 4 * NQUADS * (l + 1))
                link(v.tensor_scalar(recip, sums[:, :, 0:H], 1e-30, None, ALU.max))
                link(v.reciprocal(recip, recip))
                messages = sums[:, :, H:SUMC].rearrange("p c (h o) -> p c h o", h=H)
                v.tensor_tensor(messages, messages, bc(recip, 3, HS), ALU.mult).then_inc(agg_ready, 1)

            typed(0)
            for l in range(L):
                build_table(l)
                attend(l)
                typed(l + 1)


_INS = ["x", "src", "dst", "edge_type_32", "node_type_16", "L0_gnn_Wk", "L0_gnn_Wq", "L0_gnn_Wv", "L0_gnn_Wa", "L0_gnn_Watt",
        "L0_gnn_Wmsg", "L0_gnn_pri", "L0_gnn_skip", "L0_gnn_ln_g", "L0_gnn_ln_b", "L0_gnn_ff_w", "L0_gnn_ff_b"]


def kernel(**inputs):
    import numpy as _np
    import concourse.bacc as _bacc
    from concourse import mybir as _mybir
    from concourse.bass_utils import run_bass_kernel_spmd as _run

    nc = _bacc.Bacc("TRN2", target_bir_lowering=False, num_devices=1)
    arrays, args = {}, []
    for name in _INS:
        a = _np.ascontiguousarray(inputs[name])
        arrays[f"in_{name}_dram"] = a
        args.append(nc.dram_tensor(f"in_{name}_dram", a.shape, _mybir.dt.from_np(a.dtype), kind="ExternalInput").ap())
    args.append(nc.dram_tensor("out_dram", (N, D), _mybir.dt.float32, kind="ExternalOutput").ap())
    gnn_kernel(nc, *args)
    r = _run(nc, [arrays], core_ids=[0])
    return r.results[0]["out_dram"]
```

```python
import numpy as np
import concourse.bass as bass
from concourse import mybir
from contextlib import ExitStack

P = 128
N, E, D, H, HS, RT, NT, L = 6250, 100000, 128, 8, 16, 32, 16, 2
NTILES = -(-N // P)
NPAD = NTILES * P
SORTED_TILES = NTILES - 1 + NT
GROUP = 4
GROUPS = SORTED_TILES // GROUP
EPP = -(-E // P)
ETILES = EPP
EROWS = ETILES + 2
BLOCK = 32
NBLOCKS = -(-(ETILES + NTILES - 1) // BLOCK)
SLOTS = NBLOCKS * BLOCK
SCOLS = -(-SLOTS // P)
CHUNKS = P // H
PER_CHUNK = BLOCK // CHUNKS
CLEN = PER_CHUNK * P
QUAD = 4
QPB = BLOCK // QUAD
NQUADS = NBLOCKS * QPB
FIRST_WEIGHED = 4
FIRST_SUMMED = FIRST_WEIGHED + 1
BIG = 1.0e30
NO_NODE = 8192.0
NO_DST = 20000.0
EPS = 1e-5
X_PART = [0, 0, 0, 1, 1, 1, 2, 2]
W_PART = [0, 1, 2, 0, 1, 2, 0, 1]
PARTS = len(X_PART)
Z_BANK, OUT_BANK = (1, 7), (3, 4)
TABLE_ROW = 2 * D
PREP_COLUMNS = 11264
RHS0 = D - H
SUMC = H + D


def gnn_kernel(nc, x, src, dst, etype, ntype, Wk, Wq, Wv, Wa, Watt, Wmsg, pri, skip, ln_g, ln_b, ff_w, ff_b, out):
    F32, I32, BF16 = mybir.dt.float32, mybir.dt.int32, mybir.dt.bfloat16
    ALU, ACT, AX = mybir.AluOpType, mybir.ActivationFunctionType, mybir.AxisListType
    PE_, DVE_ = mybir.EngineType.PE, mybir.EngineType.DVE

    ctx = ExitStack()
    with ctx:
        def sb(name, shape, dt):
            return ctx.enter_context(nc.sbuf_tensor(name, shape, dt))

        def sem(name):
            return ctx.enter_context(nc.semaphore(name))

        def dram(name, shape, dt):
            return nc.dram_tensor(name, shape, dt).ap()

        def bc(ap, axis, n):
            u = ap.unsqueeze(axis)
            shape = list(u.shape)
            shape[axis] = n
            return u.to_broadcast(shape)

        table = dram("relation_table", [NPAD * RT, TABLE_ROW], F32)
        qkv_dram = dram("qkv_rows", [NPAD, 3 * D], F32)
        agg_dram = dram("aggregated_rows", [NPAD, D], F32)
        x_sorted = dram("x_sorted", [SORTED_TILES * P, D], F32)
        h_sorted = dram("h_sorted", [SORTED_TILES * P, D], F32)
        node_of_place = dram("node_of_place", [P * SORTED_TILES, 1], I32)
        key_flat = dram("edge_keys", [EROWS * P], F32)
        dst_flat = dram("edge_dst", [EROWS * P + 2], F32)
        edge_rows = dram("edge_rows", [EROWS, 4 * P], F32)
        flag_rows = dram("segment_flags", [2, SCOLS * P, P], F32)
        w_parts = dram("relation_weight_parts", [L, 2, 3, H, HS, RT * HS], BF16)

        ident = sb("ident", [P, P], F32)
        identb = sb("identb", [P, P], BF16)
        ones = sb("ones", [P, P], F32)
        iota_free = sb("iota_free", [P, P], F32)
        key_of = sb("key_of", [P, SCOLS * P], F32)
        minus_dst = sb("minus_dst", [P, SCOLS * P], F32)
        invalid = sb("invalid", [P, SCOLS * P], F32)
        crossing = sb("crossing", [1, SCOLS * P // BLOCK], F32)
        dst_tile = sb("dst_tile", [1, SCOLS * P], I32)
        gather_node = sb("gather_node", [P, SORTED_TILES], I32)
        scatter_node = sb("scatter_node", [P, SORTED_TILES], I32)
        tile_type = sb("tile_type", [1, SORTED_TILES], I32)
        type_of_tile = sb("type_of_tile", [P, SORTED_TILES], F32)
        half_alpha = sb("half_alpha", [P, SORTED_TILES], F32)
        one_less_alpha = sb("one_less_alpha", [P, SORTED_TILES], F32)
        minus_half = sb("minus_half", [P, 2, GROUP], F32)
        alpha_t = sb("alpha_t", [P, NT], F32)
        type_no = sb("type_no", [P, NT], F32)
        row_const = sb("row_const", [P, 3, D], F32)

        sums = sb("sums", [P, NTILES, SUMC], F32)
        region_q = sb("region_q", [P, NTILES * 3 * D], BF16)
        region_a = sb("region_a", [P, 2 * BLOCK * TABLE_ROW], F32)
        region_b = sb("region_b", [P, 2 * BLOCK * P], F32)

        q_parts = region_q[:, :].rearrange("p (c k d) -> p c k d", c=NTILES, k=3)
        wqf = region_q[:, :].bitcast(F32)
        w_qkv = wqf[:, 0:NT * 3 * D].rearrange("p (t n) -> p t n", t=NT)
        w_a = wqf[:, NT * 3 * D:NT * 3 * D + NT * D].rearrange("p (t n) -> p t n", t=NT)
        w_ff = wqf[:, NT * 4 * D:NT * 4 * D + D]

        rows = region_a[:, :].rearrange("p (r s n) -> p r s n", r=2, s=BLOCK)
        onehots = region_b[:, :].rearrange("p (r s n) -> p r s n", r=2, s=BLOCK)

        stage = region_a[:, :].rearrange("p (r t n) -> p r t n", r=2, t=RT)
        rb16 = region_b[:, :].bitcast(BF16)
        spare = sums[:, :].rearrange("p c n -> p (c n)")
        kvq = spare[:, 0:12 * D].rearrange("p (r n) -> p r n", r=4)
        resid1, resid2 = spare[:, 12 * D:15 * D], spare[:, 15 * D:18 * D]
        rel_f = spare[:, 0:L * 1024].rearrange("p (l n) -> p l n", l=L)
        rel_r = spare[:, 2048:3072]
        rel_p = spare[:, 3072:6144].bitcast(BF16).rearrange("p (l k w n) -> p l k w n", l=L, k=2, w=3)
        rel_pri = spare[:, 6144:6208].rearrange("p (l t) -> p l t", l=L)
        w_rel = rb16[:, 0:8192].rearrange("p (k n) -> p k n", k=2 * H)
        x_spread = rb16[:, 8192:12288].rearrange("p (r k w d) -> p r k w d", r=2, k=2 * H, w=PARTS)
        x_spreadT = rb16[:, 12288:16384].rearrange("p (r k n) -> p r k n", r=2, k=2 * H)

        def take(base, w, shape):
            v = region_a[:, base:base + w]
            return v.rearrange("p (r a b) -> p r a b", r=2, a=shape[0]), base + w

        o = 0
        g_in, o = take(o, 2 * GROUP * D, (GROUP, D))
        g_res, o = take(o, 2 * GROUP * D, (GROUP, D))
        g_x, o = take(o, 2 * GROUP * D, (GROUP, D))
        g_inT, o = take(o, 2 * GROUP * D, (GROUP, D))
        g_th, o = take(o, 2 * GROUP * D, (GROUP, D))
        g_h, o = take(o, 2 * GROUP * D, (GROUP, D))
        tile_is_type = region_a[:, o:o + SORTED_TILES * NT].rearrange("p (i t) -> p i t", t=NT)
        o = PREP_COLUMNS
        g_hn, o = take(o, 2 * GROUP * D, (GROUP, D))
        g_hnT, o = take(o, 2 * GROUP * D, (GROUP, D))
        g_out, o = take(o, 2 * GROUP * 3 * D, (GROUP, 3 * D))
        step_mark = sb("step_mark", [1, 1], F32)
        bn_in = sb("bn_in", [P, 2, GROUP, 6], F32)
        mean_var = sb("mean_var", [P, 2, GROUP, 2], F32)
        var_eps = sb("var_eps", [P, 2, 2, GROUP], F32)
        rstd = sb("rstd", [P, 2, 2, GROUP], F32)
        out_mean_var = sb("out_mean_var", [P, 2, GROUP, 2], F32)
        out_shift = sb("out_shift", [P, 2, GROUP], F32)

        block_keys = sb("block_keys", [P, 2, BLOCK], I32)
        onehotT = sb("onehotT", [P, 2, QUAD, P], BF16)
        prod = sb("prod", [P, 2, QUAD, D], F32)
        score = sb("score", [P, 2, BLOCK, H], F32)
        masked = sb("masked", [P, PER_CHUNK, CHUNKS, H], F32)
        flags = sb("flags", [P, 2, 2, CLEN], F32)
        first_seg = sb("first_seg", [P, CLEN], F32)
        last_seg = sb("last_seg", [P, CLEN], F32)
        fwd = sb("fwd", [P, CLEN], F32)
        bwd = sb("bwd", [P, CLEN], F32)
        edge_max = sb("edge_max", [P, CLEN], F32)
        below_max = sb("below_max", [P, BLOCK, H], F32)
        carry_in = sb("carry_in", [1, 2, 2, H, CHUNKS + 1], F32)
        carry_out = sb("carry_out", [1, 2, H, CHUNKS + 1], F32)
        carry_rows = sb("carry_rows", [1, 2, CHUNKS, H], F32)
        chunk_carry = sb("chunk_carry", [P, 2], F32)
        carried = sb("carried", [1, H], F32)
        lower = sb("lower", [1, H], F32)
        cross_hot = sb("cross_hot", [1, P], F32)
        rescale = sb("rescale", [P, H], F32)
        recip = prod[:, :].rearrange("p r s d -> p (r s d)")[:, 0:NTILES * H].rearrange("p (c h) -> p c h", h=H)

        bank = [ctx.enter_context(nc.psum_tensor(f"bank{i}", [P, 512], F32)) for i in range(8)]

        pool_const = sem("pool_const")
        pool_chain = sem("pool_chain")
        dve_chain = sem("dve_chain")
        pads_set = sem("pads_set")
        type_in, edge_in = sem("type_in"), sem("edge_in")
        counted, placed_psum = sem("counted"), sem("placed_psum")
        place_ready, place_init, place_done = sem("place_ready"), sem("place_init"), sem("place_done")
        place_loaded = sem("place_loaded")
        flat_ready, flat_stored, rows_built = sem("flat_ready"), sem("flat_stored"), sem("rows_built")
        bound_counted, bound_psum = sem("bound_counted"), sem("bound_psum")
        slot_rows_ready, slot_rows_in = sem("slot_rows_ready"), sem("slot_rows_in")
        slot_calc, slot_T, slot_copied, flags_stored = sem("slot_calc"), sem("slot_T"), sem("slot_copied"), sem("flags_stored")
        prep_done, nodes_ready = sem("prep_done"), sem("nodes_ready")
        layer_const_in, alpha_exp, layer_const_ready = sem("layer_const_in"), sem("alpha_exp"), sem("layer_const_ready")
        weights_in = sem("weights_in")
        rel_in, rel_split, parts_stored, w_rel_in = sem("rel_in"), sem("rel_split"), sem("parts_stored"), sem("w_rel_in")
        pad_rows_stored = sem("pad_rows_stored")
        gathered = [sem(f"gathered{i}") for i in range(2)]
        res_in = [sem(f"res_in{i}") for i in range(2)]
        x_in = [sem(f"x_in{i}") for i in range(2)]
        stored = [sem(f"stored{i}") for i in range(2)]
        scattered = [sem(f"scattered{i}") for i in range(2)]
        inT_psum, inT_ready, z_psum, tanh_done = sem("inT_psum"), sem("inT_ready"), sem("z_psum"), sem("tanh_done")
        var_ready, out_var_ready, rstd_ready = sem("var_ready"), sem("out_var_ready"), sem("rstd_ready")
        hn_ready, res_scaled = sem("hn_ready"), sem("res_scaled")
        hnT_psum, hnT_ready, out_psum, out_ready = sem("hnT_psum"), sem("hnT_ready"), sem("out_psum"), sem("out_ready")
        kvq_in = [sem(f"kvq_in{i}") for i in range(4)]
        spread_ready, spread_T, spreadT_ready = sem("spread_ready"), sem("spread_T"), sem("spreadT_ready")
        table_psum, stage_act, stage_dve = sem("table_psum"), sem("stage_act"), sem("stage_dve")
        table_stored = [sem(f"table_stored{i}") for i in range(2)]
        rows_in = [sem(f"rows_in{i}") for i in range(QPB)]
        onehot_ready, onehotT_psum, onehotT_ready = sem("onehot_ready"), sem("onehotT_psum"), sem("onehotT_ready")
        q_psum, prod_ready, score_ready = sem("q_psum"), sem("prod_ready"), sem("score_ready")
        flags_in = [sem(f"flags_in{i}") for i in range(2)]
        masked_ready, masked_T, scans_ready = sem("masked_ready"), sem("masked_T"), sem("scans_ready")
        chunk_rows, carry_ready, carry_T, max_ready, max_T = (sem("chunk_rows"), sem("carry_ready"), sem("carry_T"),
                                                              sem("max_ready"), sem("max_T"))
        below_ready, exp_ready, lower_ready, rescale_psum = (sem("below_ready"), sem("exp_ready"), sem("lower_ready"),
                                                             sem("rescale_psum"))
        cross_ready = sem("cross_ready")
        weighted, sum_psum, sum_added = sem("weighted"), sem("sum_psum"), sem("sum_added")
        z_used, norm_ready = sem("z_used"), sem("norm_ready")
        act_chain, q_split = sem("act_chain"), sem("q_split")
        keys_ready, passed = sem("keys_ready"), sem("passed")
        agg_ready, agg_stored = sem("agg_ready"), sem("agg_stored")

        pa = region_a
        src_i = pa[:, 0:EPP].bitcast(I32)
        typ_i = pa[:, 800:800 + EPP].bitcast(I32)
        dst_i = pa[:, 1600:1600 + EPP].bitcast(I32)
        key_f = pa[:, 2400:2400 + EPP]
        dst_f = pa[:, 3200:3200 + EPP]
        junk = pa[:, 4000:4000 + EPP]
        junk_b = pa[:, 5632:5632 + EPP]
        bounds = pa[:, 4800:4800 + NTILES - 1]
        starts = pa[:, 4864:4864 + NTILES - 1]
        starts_i = pa[:, 4928:4928 + NTILES - 1].bitcast(I32)
        slot_cmp = pa[:, 5000:5000 + SCOLS * (NTILES - 1)].rearrange("p (c d) -> p c d", c=SCOLS)
        slot_no = pa[:, 5400:5400 + SCOLS]
        slot_dt = pa[:, 5408:5408 + SCOLS]
        slot_et = pa[:, 5416:5416 + SCOLS]
        slot_et_i = pa[:, 5424:5424 + SCOLS].bitcast(I32)
        slot_base = pa[:, 5432:5432 + SCOLS]
        cross_col = pa[:, 5440:5440 + SCOLS]
        pad_lo = pa[:, 5500:5500 + 2]
        srow = pa[:, 5632:5632 + SCOLS * 512].rearrange("p (c k e) -> p c k e", c=SCOLS, k=4)
        s_loc = pa[:, 9216:9216 + SCOLS * P].rearrange("p (c e) -> p c e", c=SCOLS)
        s_valid = pa[:, 10112:10112 + SCOLS * P].rearrange("p (c e) -> p c e", c=SCOLS)
        s_a = pa[:, 0:SCOLS * P].rearrange("p (c e) -> p c e", c=SCOLS)
        s_flag = pa[:, SCOLS * P:3 * SCOLS * P].rearrange("p (k c e) -> p k c e", k=2, c=SCOLS)
        pb = region_b
        upper = pb[:, 0:P]
        iota_i = pb[:, 128:256].bitcast(I32)
        part_i = pb[:, 256:257].bitcast(I32)
        part_f = pb[:, 257:258]
        slot_i = pb[:, 264:264 + SCOLS].bitcast(I32)
        node_i = pb[:, 272:272 + NTILES].bitcast(I32)
        nt_i = pb[:, 328:328 + NTILES].bitcast(I32)
        nt_f = pb[:, 384:384 + NTILES]
        onehot_t = pb[:, 512:512 + NT * NTILES].rearrange("p (t c) -> p t c", t=NT)
        keep = pb[:, 1300:1300 + NT * NTILES].rearrange("p (t c) -> p t c", t=NT)
        ranks = pb[:, 2100:2100 + NT * NTILES].rearrange("p (t c) -> p t c", t=NT)
        tot = pb[:, 2900:2916]
        tot_i = pb[:, 2916:2932].bitcast(I32)
        tiles_t = pb[:, 2932:2948]
        first_tile = pb[:, 2948:2964]
        base_t = pb[:, 2964:2980]
        pos = pb[:, 2980:2980 + NTILES]
        pos_i = pb[:, 3032:3032 + NTILES].bitcast(I32)
        pos_lo = pb[:, 3084:3084 + NTILES].bitcast(I32)
        pos_hi = pb[:, 3136:3136 + NTILES].bitcast(I32)
        pos_lof = pb[:, 3188:3188 + NTILES]
        is_pad = pb[:, 3240:3240 + NTILES]
        place_i = pb[:, 3292:3292 + NTILES].bitcast(I32)
        no_node = pb[:, 3344:3344 + SORTED_TILES].bitcast(I32)
        tile_no = pb[:, 3408:3408 + SORTED_TILES]
        type_f = pb[:, 3472:3472 + SORTED_TILES]
        type_cmp = pb[:, 3584:3584 + SORTED_TILES * NT].rearrange("p (i t) -> p i t", t=NT)
        zeros = pb[:, 4608:4608 + 3 * D]
        pad_dst = pb[:, 5000:5002]
        pad_key = pb[:, 5004:5006]
        before_first = pb[:, 5008:5009]
        node_f = pb[:, 5016:5016 + SORTED_TILES]
        ALL_FULL = E // EPP
        LAST_EDGES = E - ALL_FULL * EPP
        NFULL = N // NTILES
        LAST_NODES = N - NFULL * NTILES

        block = ctx.enter_context(nc.Block())

        def shifted(i, par, n):
            return i + (par + n) // 2, (par + n) % 2

        def is_pair(i):
            return not isinstance(i, int) or 0 <= i < GROUPS // 2

        def late_quad(b, par, q, first):
            return (b - 1, 1 - par, q - first) if q >= first else (b - 2, par, q - first + QPB)

        def is_block(b):
            return not isinstance(b, int) or 0 <= b < NBLOCKS

        def wait(eng, semaphore, value):
            if not (isinstance(value, int) and value <= 0):
                eng.wait_ge(semaphore, value)

        class Chain:

            def __init__(self, eng, semaphore):
                self.eng, self.semaphore, self.n = eng, semaphore, 0

            def step(self, instruction):
                instruction.then_inc(self.semaphore, 1)
                self.n = self.n + 1
                return self.n

            def wait(self, upto=None):
                self.eng.wait_ge(self.semaphore, self.n if upto is None else upto)

        def repeat(eng, count, body, chain=None):
            start = chain.n if chain else 0
            body(0)
            per = (chain.n - start) if chain else 0
            if count > 1:
                with eng.Fori(1, count) as i:
                    if chain:
                        chain.n = i * per + start
                    body(i)
                if chain:
                    chain.n = start + per * count

        def group_rows(array, g):
            return array[bass.ds(g * GROUP * P, GROUP * P), :].rearrange("(t p) d -> p t d", p=P)

        HALF_GROUPS = GROUPS // 2
        AGG_PARTS = [slice(k * NTILES // 4, (k + 1) * NTILES // 4) for k in range(4)]
        FOURS = NTILES // 4

        def stage_uses(l, i, k):
            return 2 * i + (k // 2 + l * (NTILES // 2 + 1 - k % 2))

        def kvq_uses(l, i, k):
            return i + l * (FOURS + (k == 0))

        @block.sync
        def _(sp):
            def load_weights(ph):
                if ph > 0:
                    for half in (slice(0, NT // 2), slice(NT // 2, NT)):
                        sp.dma_start(w_a[:, half, :], Wa[ph - 1, half].rearrange("t d o -> d t o")).then_inc(weights_in, 16)
                    sp.dma_start(row_const[:, 0, :], ln_g[ph - 1:ph, :].to_broadcast([P, D])).then_inc(layer_const_in, 16)
                    sp.dma_start(row_const[:, 1, :], ln_b[ph - 1:ph, :].to_broadcast([P, D])).then_inc(layer_const_in, 16)
                    sp.dma_start(row_const[:, 2, :], ff_b.unsqueeze(0).to_broadcast([P, D])).then_inc(layer_const_in, 16)
                    sp.dma_start(alpha_t[:, :], skip[ph - 1:ph, :].to_broadcast([P, NT])).then_inc(layer_const_in, 16)
                if ph < 2:
                    for k, w in enumerate((Wq, Wk, Wv)):
                        for half in (slice(0, NT // 2), slice(NT // 2, NT)):
                            sp.dma_start(w_qkv[:, half, k * D:(k + 1) * D], w[ph, half].rearrange("t d o -> d t o")).then_inc(weights_in, 16)
                else:
                    sp.dma_start(w_ff, ff_w).then_inc(weights_in, 16)

            sp.wait_ge(pads_set, 1)
            sp.dma_start(nt_i[0:NFULL, :], ntype[0:NFULL * NTILES].rearrange("(p c) -> p c", c=NTILES)).then_inc(type_in, 16)
            sp.dma_start(nt_i[NFULL:P, 0:LAST_NODES], ntype[NFULL * NTILES:N].unsqueeze(0)).then_inc(type_in, 16)
            for buf, source in ((src_i, src), (typ_i, etype), (dst_i, dst)):
                sp.dma_start(buf[0:ALL_FULL, :], source[0:ALL_FULL * EPP].rearrange("(p c) -> p c", c=EPP)).then_inc(edge_in, 16)
                sp.dma_start(buf[ALL_FULL:P, 0:LAST_EDGES], source[ALL_FULL * EPP:E].unsqueeze(0)).then_inc(edge_in, 16)
            sp.dma_start(node_of_place.rearrange("(p i) o -> p (i o)", p=P), no_node).then_inc(place_init, 16)
            sp.dma_start(qkv_dram[N:NPAD, :], zeros[0:NPAD - N, :]).then_inc(pad_rows_stored, 16)
            sp.dma_start(dst_flat[0:1].unsqueeze(0), before_first[0:1, :]).then_inc(flat_stored, 16)
            sp.dma_start(dst_flat[1 + P * EPP:1 + EROWS * P].rearrange("(p c) -> p c", c=2), pad_dst).then_inc(flat_stored, 16)
            sp.dma_start(dst_flat[1 + EROWS * P:2 + EROWS * P].unsqueeze(0), pad_dst[0:1, 0:1]).then_inc(flat_stored, 16)
            sp.dma_start(key_flat[P * EPP:EROWS * P].rearrange("(p c) -> p c", c=2), pad_key).then_inc(flat_stored, 16)
            load_weights(0)
            sp.wait_ge(flat_ready, 1)
            sp.dma_start(key_flat[0:P * EPP].rearrange("(p c) -> p c", c=EPP), key_f).then_inc(flat_stored, 16)
            sp.dma_start(dst_flat[1:1 + P * EPP].rearrange("(p c) -> p c", c=EPP), dst_f).then_inc(flat_stored, 16)
            sp.wait_ge(flat_stored, 96)
            for k, flat in enumerate((key_flat[0:EROWS * P], dst_flat[1:1 + EROWS * P], dst_flat[0:EROWS * P],
                                      dst_flat[2:2 + EROWS * P])):
                sp.dma_start(edge_rows[:, k * P:(k + 1) * P], flat.rearrange("(r e) -> r e", e=P)).then_inc(rows_built, 16)
            sp.wait_ge(place_done, 16 * NTILES)
            sp.dma_start(scatter_node[:, :], node_of_place.rearrange("(p i) o -> p (i o)", p=P)).then_inc(place_loaded, 16)
            sp.wait_ge(rel_split, L)
            for l in range(L):
                for k in range(2):
                    for w in range(3):
                        sp.dma_start(w_parts[l, k, w].rearrange("h d n -> (h d) n"), rel_p[:, l, k, w, :]).then_inc(parts_stored, 16)

            def relation_weights(l):
                for k in range(2):
                    for s in range(PARTS):
                        sp.dma_start(w_rel[s * HS:(s + 1) * HS, k * H:(k + 1) * H, :],
                                     w_parts[l, k, W_PART[s]].rearrange("h d n -> d h n")).then_inc(w_rel_in, 16)

            def typed(ph):
                if ph == 1:
                    relation_weights(1)

                def load_res(i, par):
                    sp.dma_start(g_res[:, par], group_rows(x_sorted if ph == 1 else h_sorted, 2 * i + par)).then_inc(res_in[par], 16)

                def load_x(i, par):
                    sp.dma_start(g_x[:, par], group_rows(x_sorted, 2 * i + par)).then_inc(x_in[par], 16)

                for par in range(2):
                    if ph > 0:
                        load_res(0, par)
                    if ph == 2:
                        load_x(0, par)

                def store_rows(i, par):
                    sp.wait_ge(hn_ready, 2 * i + par + 1)
                    sp.dma_start(group_rows(h_sorted, 2 * i + par), g_hn[:, par]).then_inc(stored[par], 16)

                def groups(i):
                    for par in range(2):
                        g = 2 * i + par
                        if ph == 0:
                            sp.wait_ge(gathered[par], i * 64 + 64)
                            sp.dma_start(group_rows(x_sorted, g), g_hn[:, par]).then_inc(stored[par], 16)
                        more = ph > 0 and not (isinstance(i, int) and i == HALF_GROUPS - 1)
                        if more:
                            sp.wait_ge(var_ready, g + ((ph - 1) * GROUPS + 1))
                            load_res(i + 1, par)
                        before = shifted(i, par, -1)
                        if ph == 1 and is_pair(before[0]):
                            store_rows(*before)
                        if ph == 2 and is_pair(shifted(i, par, -2)[0]):
                            sp.wait_ge(out_psum, g + (2 * GROUPS - 1))
                            load_x(i, par)

                if ph == 0:
                    groups(0)
                    sp.wait_ge(slot_calc, 1)
                    for k in range(2):
                        sp.dma_start(flag_rows[k].rearrange("(c p) e -> p c e", p=P), s_flag[:, k]).then_inc(flags_stored, 16)
                    with sp.Fori(1, HALF_GROUPS) as i:
                        groups(i)
                    sp.wait_ge(parts_stored, 16 * 6 * L)
                    sp.wait_ge(prep_done, 1)
                    relation_weights(0)
                else:
                    repeat(sp, HALF_GROUPS - 1, groups)
                    groups(HALF_GROUPS - 1)
                if ph == 1:
                    store_rows(HALF_GROUPS - 1, 1)

            def build_table(l):
                for par in range(2):
                    sp.wait_ge(scattered[par], 64 * HALF_GROUPS * (l + 1))
                    sp.wait_ge(stored[par], 16 * HALF_GROUPS * (l + 1))
                if l == 0:
                    sp.wait_ge(pad_rows_stored, 16)

                def load(i, k):
                    sp.dma_start(kvq[:, k], qkv_dram[bass.ds((4 * i + k) * P, P), :]).then_inc(kvq_in[k], 16)

                def tile(i, k, more):
                    c = 4 * i + k
                    sp.wait_ge(stage_act, c * H + (l * NTILES + 1) * H)
                    sp.wait_ge(stage_dve, c * H + (l * NTILES + 1) * H)
                    sp.dma_start(table[bass.ds(c * P * RT, P * RT), :].rearrange("(p t) n -> p t n", t=RT),
                                 stage[:, k % 2]).then_inc(table_stored[k % 2], 16)
                    if more:
                        load(i + 1, k)

                for k in range(4):
                    load(0, k)

                def four(i):
                    for k in range(4):
                        tile(i, k, True)

                repeat(sp, FOURS - 1, four)
                for k in range(4):
                    tile(FOURS - 1, k, k == 0)
                tile(FOURS, 0, False)

            def attend(l):
                def load_flags(i, par):
                    for k in range(2):
                        rows_ = flag_rows[k, bass.ds((2 * i + par) * BLOCK, BLOCK), :]
                        source = bc(rows_.rearrange("(j i) e -> j (i e)", i=PER_CHUNK), 1, H)
                        sp.dma_start(flags[:, par, k, :], source).then_inc(flags_in[par], 16)

                def blocks(i):
                    for par in range(2):
                        b = 2 * i + par
                        wait(sp, scans_ready, b + (l * NBLOCKS - 1))
                        load_flags(i, par)

                repeat(sp, NBLOCKS // 2, blocks)
                sp.wait_ge(q_psum, NQUADS * (l + 1))
                load_weights(l + 1)
                for k, part in enumerate(AGG_PARTS):
                    sp.wait_ge(agg_ready, len(AGG_PARTS) * l + k + 1)
                    sp.dma_start(agg_dram.rearrange("(c p) d -> p c d", p=P)[:, part], sums[:, part, H:SUMC]).then_inc(agg_stored, 16)

            typed(0)
            for l in range(L):
                build_table(l)
                attend(l)
                typed(l + 1)
            for par in range(2):
                sp.wait_ge(scattered[par], 64 * HALF_GROUPS * (L + 1))

        @block.gpsimd
        def _(pool):
            chain = Chain(pool, pool_chain)

            nc.gpsimd.iota(iota_i, [[1, P]], channel_multiplier=0).then_inc(pool_const, 1)
            nc.gpsimd.iota(part_i, [[0, 1]], channel_multiplier=1).then_inc(pool_const, 1)
            nc.gpsimd.iota(slot_i, [[P, SCOLS]], channel_multiplier=1).then_inc(pool_const, 1)
            nc.gpsimd.iota(node_i, [[1, NTILES]], channel_multiplier=NTILES).then_inc(pool_const, 1)
            pool.wait_ge(place_ready, 1)
            pool.wait_ge(place_init, 16)
            pool.wait_ge(pool_const, 4)
            for c in range(NTILES):
                pool.indirect_dma_start(out=node_of_place, out_offset=bass.IndirectOffsetOnAxis(ap=place_i[:, c:c + 1], axis=0),
                                        in_=node_i[:, c:c + 1], in_offset=None,
                                        bounds_check=P * SORTED_TILES - 1, oob_is_err=False).then_inc(place_done, 16)
            pool.wait_ge(slot_rows_ready, 1)
            pool.wait_ge(rows_built, 64)
            for c in range(SCOLS):
                pool.indirect_dma_start(out=srow[:, c].rearrange("p k e -> p (k e)"), out_offset=None, in_=edge_rows,
                                        in_offset=bass.IndirectOffsetOnAxis(ap=slot_et_i[:, c:c + 1], axis=0)).then_inc(slot_rows_in, 16)
            pool.wait_ge(nodes_ready, 1)

            def typed(ph):
                if ph > 0:
                    pool.wait_ge(agg_stored, 16 * len(AGG_PARTS) * ph)

                def gather(i, par):
                    g = 2 * i + par
                    into = g_in if ph > 0 else g_hn
                    if ph == 0:
                        wait(pool, hnT_psum, g - 1)
                        wait(pool, stored[par], i * 16)
                    else:
                        wait(pool, inT_psum, g + ((ph - 1) * GROUPS - 1))
                    for t in range(GROUP):
                        pool.indirect_dma_start(out=into[:, par, t], out_offset=None, in_=x if ph == 0 else agg_dram,
                                                in_offset=bass.IndirectOffsetOnAxis(ap=gather_node[:, g * GROUP + t:g * GROUP + t + 1], axis=0)
                                                ).then_inc(gathered[par], 16)

                def power(g):
                    layer, output = g + 2 < GROUPS, ph == 2 and 0 <= g < GROUPS
                    if layer:
                        pool.wait_ge(var_ready, g + 2 + ((ph - 1) * GROUPS + 1))
                    if output:
                        pool.wait_ge(out_var_ready, g + 1)
                    kinds = slice(0 if layer else 1, 2 if output else 1)
                    if layer or output:
                        nc.gpsimd.tensor_tensor(rstd[:, g % 2, kinds], var_eps[:, g % 2, kinds], minus_half[:, kinds], ALU.pow).then_inc(rstd_ready, 1)

                def scatter(g):
                    pool.wait_ge(out_ready, g + (ph * GROUPS + 1))
                    for t in range(GROUP):
                        source = g_out[:, g % 2, t] if ph < 2 else g_out[:, g % 2, t, 0:D]
                        n = g * GROUP + t
                        pool.indirect_dma_start(out=qkv_dram if ph < 2 else out,
                                                out_offset=bass.IndirectOffsetOnAxis(ap=scatter_node[:, n:n + 1], axis=0),
                                                in_=source, in_offset=None, bounds_check=N - 1, oob_is_err=False
                                                ).then_inc(scattered[g % 2], 16)

                lead = 4 if ph > 0 else 2
                for g in range(lead):
                    gather(g // 2, g % 2)
                if ph > 0:
                    power(-2)
                    power(-1)
                for g in range(GROUPS + 2):
                    if g + lead < GROUPS:
                        gather((g + lead) // 2, (g + lead) % 2)
                    if 0 <= g - ph < GROUPS:
                        scatter(g - ph)
                    if ph > 0:
                        power(g)

            def build_table(l):
                pool.wait_ge(prep_done, 1)

                def tile(i, k):
                    c = 4 * i + k
                    par = k % 2
                    pool.wait_ge(kvq_in[k], 16 * i + 16 * kvq_uses(l, 0, k) + 16)
                    wait(pool, spread_T, 2 * c + (2 * l * NTILES - 2))
                    kv = kvq[:, k, D:3 * D].rearrange("p (k d) -> p k d", d=HS)
                    r1 = resid1[:, D:3 * D].rearrange("p (k d) -> p k d", d=HS)
                    r2 = resid2[:, D:3 * D].rearrange("p (k d) -> p k d", d=HS)
                    pool.sem_inc(passed, 1)
                    chain.step(nc.gpsimd.tensor_copy(x_spread[:, par, :, 0:3, :], bc(kv, 2, 3)))
                    chain.wait()
                    chain.step(nc.gpsimd.tensor_tensor(r1, kv, x_spread[:, par, :, 0, :], ALU.subtract))
                    chain.wait()
                    pool.sem_inc(passed, 1)
                    chain.step(nc.gpsimd.tensor_copy(x_spread[:, par, :, 3:6, :], bc(r1, 2, 3)))
                    chain.wait()
                    chain.step(nc.gpsimd.tensor_tensor(r2, r1, x_spread[:, par, :, 3, :], ALU.subtract))
                    chain.wait()
                    pool.sem_inc(passed, 1)
                    nc.gpsimd.tensor_copy(x_spread[:, par, :, 6:8, :], bc(r2, 2, 2)).then_inc(spread_ready, 1)

                def four(i):
                    for k in range(4):
                        tile(i, k)

                repeat(pool, FOURS, four, chain)
                tile(FOURS, 0)

            def attend(l):
                for par in range(2):
                    pool.wait_ge(table_stored[par], 16 * stage_uses(l + 1, 0, par))

                def gather(b, par, q):
                    quad = b * QPB + (l * NQUADS + q)
                    wait(pool, prod_ready, quad - (QPB - 1))
                    if not (isinstance(b, int) and b < 2):
                        pool.wait_ge(sum_psum, 2 * quad - 30)
                    if q == 0:
                        pool.wait_ge(keys_ready, b + (l * NBLOCKS + 1))
                    pool.sem_inc(passed, 1)
                    for s in range(QUAD):
                        pool.indirect_dma_start(out=rows[:, par, q * QUAD + s], out_offset=None, in_=table,
                                                in_offset=bass.IndirectOffsetOnAxis(ap=block_keys[:, par, q * QUAD + s:q * QUAD + s + 1], axis=0)
                                                ).then_inc(rows_in[q], 16)

                for b in range(2):
                    for q in range(QPB):
                        gather(b, b, q)
                with pool.Fori(1, NBLOCKS // 2) as i:
                    for par in range(2):
                        for q in range(QPB):
                            gather(2 * i + par, par, q)

            typed(0)
            for l in range(L):
                build_table(l)
                attend(l)
                typed(l + 1)

        @block.scalar
        def _(act):
            chain = Chain(act, act_chain)

            for l in range(L):
                for k, w in enumerate((Watt, Wmsg)):
                    for h in range(H):
                        act.dma_start(rel_f[h * HS:(h + 1) * HS, l, k * RT * HS:(k + 1) * RT * HS].rearrange("d (t o) -> d t o", o=HS),
                                      w[l, h].rearrange("t d o -> d t o")).then_inc(rel_in, 16)
                for h in range(H):
                    act.dma_start(rel_pri[h * HS:(h + 1) * HS, l, :], pri[l, h:h + 1, :].to_broadcast([HS, RT])).then_inc(rel_in, 16)

            def typed(ph):
                by_tile = lambda b_: b_[:, :].rearrange("p (t d) -> p t d", t=GROUP)
                if ph > 0:
                    act.wait_ge(layer_const_in, 64 * ph)
                    nc.scalar.activation(alpha_t[:, :], alpha_t[:, :], ACT.Exp, scale=-1.0).then_inc(alpha_exp, 1)

                def project(i, par):
                    g = 2 * i + par
                    act.wait_ge(inT_psum, g + ((ph - 1) * GROUPS + 1))
                    wait(act, z_psum, g + ((ph - 1) * GROUPS - 1))
                    nc.scalar.copy(g_inT[:, par], by_tile(bank[0])).then_inc(inT_ready, 1)
                    act.wait_ge(z_psum, g + ((ph - 1) * GROUPS + 1))
                    nc.scalar.activation(g_th[:, par], by_tile(bank[Z_BANK[par]]), ACT.Tanh, scale=0.5).then_inc(tanh_done, 1)

                def scale_res(i, par):
                    g = 2 * i + par
                    act.wait_ge(res_in[par], 16 * i + (16 * (ph - 1) * HALF_GROUPS + 16))
                    act.wait_ge(layer_const_ready, ph)
                    for t in range(GROUP):
                        ins = nc.scalar.activation(g_res[:, par, t], g_res[:, par, t], ACT.Copy,
                                                   scale=one_less_alpha[:, bass.ds(g * GROUP + t, 1)])
                    ins.then_inc(res_scaled, 1)

                def produce(i, par):
                    g = 2 * i + par
                    act.wait_ge(hnT_psum, g + (ph * GROUPS + 1))
                    wait(act, out_psum, g + (ph * GROUPS - 1))
                    nc.scalar.copy(g_hnT[:, par], by_tile(bank[2])).then_inc(hnT_ready, 1)
                    if ph < 2:
                        act.wait_ge(out_psum, g + (ph * GROUPS + 1))
                        wait(act, scattered[par], 64 * i + 64 * ph * HALF_GROUPS)
                        for t in range(GROUP):
                            ins = nc.scalar.copy(g_out[:, par, t], bank[3 + t][:, 0:3 * D])
                        ins.then_inc(out_ready, 1)

                def normalise(i, par):
                    g = 2 * i + par
                    act.wait_ge(norm_ready, g + 1)
                    wait(act, scattered[par], 64 * i + 64 * 2 * HALF_GROUPS)
                    for t in range(GROUP):
                        ins = nc.scalar.activation(g_out[:, par, t, 0:D], bank[OUT_BANK[par]][:, t * D:(t + 1) * D], ACT.Identity,
                                                   scale=rstd[:, par, 1, t:t + 1], bias=out_shift[:, par, t:t + 1])
                    ins.then_inc(out_ready, 1)

                def groups(i):
                    for par in range(2):
                        coming, before = shifted(i, par, 3), shifted(i, par, -1)
                        if ph > 0 and is_pair(coming[0]):
                            project(*coming)
                        produce(i, par)
                        if ph > 0 and is_pair(coming[0]):
                            scale_res(*coming)
                        if ph == 2 and is_pair(before[0]):
                            normalise(*before)

                if ph > 0:
                    for g in range(3):
                        project(g // 2, g % 2)
                        scale_res(g // 2, g % 2)
                repeat(act, HALF_GROUPS - 2, groups)
                for i in (HALF_GROUPS - 2, HALF_GROUPS - 1):
                    groups(i)
                if ph == 2:
                    normalise(HALF_GROUPS - 1, 1)

            def build_table(l):
                def tile(i, k):
                    c = 4 * i + k
                    par = k % 2
                    for half in range(2):
                        act.wait_ge(spread_T, 2 * c + (2 * l * NTILES + half + 1))
                        wait(act, table_psum, 16 * c + (16 * l * NTILES - 16))
                        nc.scalar.copy(x_spreadT[:, par, half * H:(half + 1) * H, :],
                                       bank[half][:, :].bitcast(BF16).rearrange("p (k n) -> p k n", k=H)).then_inc(spreadT_ready, 1)
                    wait(act, table_stored[par], 32 * i + 16 * stage_uses(l, 0, k))
                    for n in range(0, 2 * H, 2):
                        act.wait_ge(table_psum, 16 * c + (16 * l * NTILES + n + 1))
                        nc.scalar.copy(stage[:, par, :, n * HS:(n + 1) * HS],
                                       bank[2 + n % 6][:, :].rearrange("p (t o) -> p t o", t=RT)).then_inc(stage_act, 1)

                def four(i):
                    for k in range(4):
                        tile(i, k)

                repeat(act, FOURS, four)
                tile(FOURS, 0)

            def attend(l):
                def keys(b, par):
                    nc.scalar.copy(block_keys[:, par, :], key_of[:, bass.ds(b * BLOCK, BLOCK)]).then_inc(keys_ready, 1)

                def mark(b, par, q):
                    quad = b * QPB + (l * NQUADS + q)
                    if not (isinstance(b, int) and b < 2):
                        act.wait_ge(sum_psum, 2 * quad - 30)
                    for s in range(QUAD):
                        chain.step(nc.scalar.activation(onehots[:, par, q * QUAD + s], iota_free[:, :], ACT.Abs,
                                                        bias=minus_dst[:, bass.ds(b * BLOCK + (q * QUAD + s), 1)]))
                    chain.wait()
                    nc.scalar.activation(onehots[:, par, q * QUAD:(q + 1) * QUAD], onehots[:, par, q * QUAD:(q + 1) * QUAD], ACT.Relu,
                                         scale=-1.0, bias=1.0).then_inc(onehot_ready, 1)

                def mark_ahead(b, par, q):
                    if q + 3 < QPB:
                        mark(b, par, q + 3)
                    elif is_block(b + 1):
                        mark(b + 1, 1 - par, q + 3 - QPB)

                def turned(b, par, q):
                    quad = b * QPB + (l * NQUADS + q)
                    act.wait_ge(onehotT_psum, quad + 1)
                    wait(act, q_psum, quad - 1)
                    nc.scalar.copy(onehotT[:, q % 2], bank[0][:, :].rearrange("p (s e) -> p s e", s=QUAD)).then_inc(onehotT_ready, 1)

                def block_of(b, par):
                    for q in range(QPB):
                        if is_block(b):
                            if q + 2 < QPB:
                                turned(b, par, q + 2)
                            elif is_block(b + 1):
                                turned(b + 1, 1 - par, q + 2 - QPB)
                            if q == 0 and is_block(b + 1):
                                wait(act, prod_ready, b * QPB + l * NQUADS)
                                keys(b + 1, 1 - par)
                        if q == 4 and is_block(b - 1):
                            before = b + (l * NBLOCKS - 1)
                            act.wait_ge(below_ready, before + 1)
                            nc.scalar.activation(rows[:, 1 - par, :, RHS0:D], below_max[:, :, :], ACT.Exp).then_inc(exp_ready, 1)
                            act.wait_ge(lower_ready, before + 1)
                            nc.scalar.activation(lower[:, :], lower[:, :], ACT.Exp).then_inc(exp_ready, 1)
                        if is_block(b):
                            mark_ahead(b, par, q)

                act.wait_ge(prep_done, 1)
                wait(act, prod_ready, l * NQUADS)
                keys(0, 0)
                act.wait_ge(table_psum, 16 * NTILES * (l + 1))
                for q in range(3):
                    mark(0, 0, q)
                for q in range(2):
                    turned(0, 0, q)
                block_of(0, 0)
                start = chain.n
                block_of(1, 1)
                block_of(2, 0)
                per = chain.n - start
                with act.Fori(1, NBLOCKS // 2 - 1) as i:
                    chain.n = i * per + start
                    block_of(2 * i + 1, 1)
                    block_of(2 * i + 2, 0)
                chain.n = start + per * (NBLOCKS // 2 - 1)
                block_of(NBLOCKS - 1, 1)
                block_of(NBLOCKS, 0)

            typed(0)
            for l in range(L):
                build_table(l)
                attend(l)
                typed(l + 1)

        @block.tensor
        def _(pe):
            pe.wait_ge(counted, 1)
            nc.tensor.matmul(bank[0][:, 0:NT], upper, ranks[:, :, NTILES - 1], start=True, stop=True)
            nc.tensor.matmul(bank[1][:, 0:NT], ones[:, :], ranks[:, :, NTILES - 1], start=True, stop=True).then_inc(placed_psum, 1)
            pe.wait_ge(bound_counted, 1)
            nc.tensor.matmul(bank[2][:, 0:NTILES - 1], ones[:, :], bounds, start=True, stop=True).then_inc(bound_psum, 1)

            def turn_slots(c):
                pe.wait_ge(slot_calc, 1)
                wait(pe, slot_copied, c)
                nc.tensor.transpose(bank[7][:, 0:P], srow[:, c, 0, :], ident[:, :])
                nc.tensor.transpose(bank[7][:, P:2 * P], s_loc[:, c, :], ident[:, :])
                nc.tensor.transpose(bank[7][:, 2 * P:3 * P], s_valid[:, c, :], ident[:, :])
                nc.tensor.matmul(bank[7][0:1, 3 * P:4 * P], cross_col[:, c:c + 1], ident[:, :], start=True, stop=True)
                nc.tensor.matmul(bank[1][0:1, 0:P], slot_dt[:, c:c + 1], ident[:, :], start=True, stop=True).then_inc(slot_T, 1)

            def typed(ph):
                pe.wait_ge(weights_in, 16 * (6, 6 + 8, 6 + 8 + 3)[ph])
                if ph == 0:
                    pe.wait_ge(nodes_ready, 1)

                def tile_types(g):
                    _, types = nc.values_load_multi_w_load_instructions(
                        tile_type[0:1, bass.ds(g * GROUP, GROUP)], engines=[PE_], min_val=0, max_val=NT - 1,
                        skip_runtime_bounds_check_because="a count of comparisons with 15 tile numbers")
                    return types

                def project(i, par):
                    g = 2 * i + par
                    types = tile_types(g)
                    pe.wait_ge(gathered[par], 64 * i + 64 * (ph * HALF_GROUPS + 1))
                    wait(pe, inT_ready, g + (ph - 1) * GROUPS)
                    for t in range(GROUP):
                        ins = nc.tensor.transpose(bank[0][:, t * P:(t + 1) * P], g_in[:, par, t], ident[:, :])
                    ins.then_inc(inT_psum, 1)
                    pe.wait_ge(inT_ready, g + ((ph - 1) * GROUPS + 1))
                    wait(pe, z_used, g + ((ph - 1) * GROUPS - 1))
                    for t in range(GROUP):
                        ins = nc.tensor.matmul(bank[Z_BANK[par]][:, t * D:(t + 1) * D], g_inT[:, par, t],
                                               w_a[:, bass.ds(types[t], 1), :].rearrange("p a n -> p (a n)"), start=True, stop=True)
                    ins.then_inc(z_psum, 1)

                def produce(i, par):
                    g = 2 * i + par
                    if ph < 2:
                        types = tile_types(g)
                    if ph > 0:
                        pe.wait_ge(hn_ready, g + ((ph - 1) * GROUPS + 1))
                    else:
                        pe.wait_ge(gathered[par], 64 * i + 64)
                    wait(pe, hnT_ready, g + ph * GROUPS)
                    for t in range(GROUP):
                        ins = nc.tensor.transpose(bank[2][:, t * P:(t + 1) * P], g_hn[:, par, t], ident[:, :])
                    ins.then_inc(hnT_psum, 1)
                    pe.wait_ge(hnT_ready, g + (ph * GROUPS + 1))
                    wait(pe, out_ready, g + ph * GROUPS if ph < 2 or (isinstance(g, int) and g == 0) else g + (ph * GROUPS - 1))
                    if ph == 2:
                        pe.wait_ge(x_in[par], 16 * i + 16)
                    for t in range(GROUP):
                        if ph < 2:
                            ins = nc.tensor.matmul(bank[3 + t][:, 0:3 * D], g_hnT[:, par, t],
                                                   w_qkv[:, bass.ds(types[t], 1), :].rearrange("p a n -> p (a n)"), start=True, stop=True)
                        else:
                            y = bank[OUT_BANK[par]][:, t * D:(t + 1) * D]
                            nc.tensor.matmul(y, g_hnT[:, par, t], w_ff, start=True, stop=False)
                            nc.tensor.matmul(y, ones[0:1, :], row_const[0:1, 2, :], start=False, stop=False)
                            ins = nc.tensor.matmul(y, ident[:, :], g_x[:, par, t], start=False, stop=True)
                    ins.then_inc(out_psum, 1)

                def groups(i):
                    for par in range(2):
                        coming = shifted(i, par, 3)
                        if ph > 0 and is_pair(coming[0]):
                            project(*coming)
                        produce(i, par)

                if ph > 0:
                    for g in range(3):
                        project(g // 2, g % 2)
                if ph == 0:
                    for g in range(GROUPS):
                        produce(g // 2, g % 2)
                        if 1 <= g <= SCOLS:
                            turn_slots(g - 1)
                else:
                    repeat(pe, HALF_GROUPS - 2, groups)
                    for i in (HALF_GROUPS - 2, HALF_GROUPS - 1):
                        groups(i)

            def build_table(l):
                pe.wait_ge(w_rel_in, 16 * 2 * PARTS * (l + 1))

                def tile(i, j):
                    c = 4 * i + j
                    par = j % 2
                    pe.wait_ge(spread_ready, c + (l * NTILES + 1))
                    for half in range(2):
                        wait(pe, spreadT_ready, 2 * c + (2 * l * NTILES + half - 1))
                        for k in range(H):
                            ins = nc.tensor.transpose(bank[half][:, :].bitcast(BF16)[:, k * P:(k + 1) * P],
                                                      x_spread[:, par, half * H + k].rearrange("p w d -> p (w d)"), identb[:, :])
                        ins.then_inc(spread_T, 1)
                    for k in range(2 * H):
                        if k % H == 0:
                            pe.wait_ge(spreadT_ready, 2 * c + (2 * l * NTILES + k // H + 1))
                        last_use = k - 6 if k >= 6 else k + 12 - 2 * H if k < 4 else k + 6 - 2 * H
                        wait(pe, stage_act if k % 2 == 0 else stage_dve, H * c + (H * l * NTILES + last_use // 2 + 1))
                        nc.tensor.matmul(bank[2 + k % 6][:, :], x_spreadT[:, par, k, :], w_rel[:, k, :], start=True, stop=True).then_inc(table_psum, 1)

                def four(i):
                    for k in range(4):
                        tile(i, k)

                repeat(pe, FOURS, four)
                tile(FOURS, 0)

            def attend(l):
                def slot_tiles(b, q):
                    _, tiles = nc.values_load_multi_w_load_instructions(
                        dst_tile[0:1, bass.ds(b * BLOCK + q * QUAD, 2 * QUAD)], engines=[PE_], min_val=0, max_val=NTILES - 1,
                        skip_runtime_bounds_check_because="a count of comparisons with 48 tile numbers")
                    return tiles

                def turn(b, par, q):
                    quad = b * QPB + (l * NQUADS + q)
                    pe.wait_ge(onehot_ready, quad + 1)
                    wait(pe, onehotT_ready, quad)
                    for s in range(QUAD):
                        ins = nc.tensor.transpose(bank[0][:, s * P:(s + 1) * P], onehots[:, par, q * QUAD + s], ident[:, :])
                    ins.then_inc(onehotT_psum, 1)

                def fetch_q(b, par, q, tiles):
                    quad = b * QPB + (l * NQUADS + q)
                    pe.wait_ge(onehotT_ready, quad + 1)
                    wait(pe, prod_ready, quad - 1)
                    for s in range(QUAD):
                        for k in range(3):
                            ins = nc.tensor.matmul(bank[1 + q % 2][:, s * D:(s + 1) * D], onehotT[:, q % 2, s],
                                                   q_parts[:, bass.ds(tiles[s], 1), k, :].rearrange("p a n -> p (a n)"),
                                                   start=(k == 0), stop=(k == 2))
                    ins.then_inc(q_psum, 1)

                def sum_quad(b, par, q):
                    quad = b * QPB + (l * NQUADS + q)
                    pe.wait_ge(weighted, quad + 1)
                    for pair in range(2):
                        wait(pe, sum_added, 4 * quad + (2 * pair - 2))
                        for s in range(2):
                            slot = q * QUAD + 2 * pair + s
                            ins = nc.tensor.matmul(bank[5 + pair][:, s * SUMC:(s + 1) * SUMC], onehots[:, par, slot],
                                                   rows[:, par, slot, RHS0:TABLE_ROW], start=True, stop=True)
                        ins.then_inc(sum_psum, 1)

                def block_of(b, par):
                    before = b + (l * NBLOCKS - 1)
                    for q in range(QPB):
                        if is_block(b - 1) and q == FIRST_SUMMED:
                            pe.wait_ge(cross_ready, before + 1)
                            nc.tensor.matmul(bank[4][:, 0:H], cross_hot[:, :], lower[:, :], start=True, stop=True).then_inc(rescale_psum, 1)
                        late = late_quad(b, par, q, FIRST_SUMMED)
                        if is_block(late[0]):
                            sum_quad(*late)
                        if is_block(b):
                            if q + 2 < QPB:
                                turn(b, par, q + 2)
                            elif is_block(b + 1):
                                turn(b + 1, 1 - par, q + 2 - QPB)
                            if q % 2 == 0:
                                tiles = slot_tiles(b, q + 1)
                            if q + 1 < QPB:
                                fetch_q(b, par, q + 1, tiles[QUAD * (q % 2):])
                            elif is_block(b + 1):
                                fetch_q(b + 1, 1 - par, 0, tiles[QUAD:])
                        if not is_block(b - 1):
                            continue
                        if q == 0:
                            pe.wait_ge(masked_ready, before + 1)
                            for n in range(PER_CHUNK):
                                ins = nc.tensor.transpose(bank[3][:, n * P:(n + 1) * P],
                                                          masked[:, n].rearrange("p j h -> p (j h)"), ident[:, :])
                            ins.then_inc(masked_T, 1)
                        if q == 1:
                            pe.wait_ge(scans_ready, before + 1)
                            by_head = ident[:, :].rearrange("p (j h) -> p h j", h=H)
                            for n, column in enumerate((fwd[:, CLEN - 1:CLEN], first_seg[:, CLEN - 1:CLEN], bwd[:, 0:1], last_seg[:, 0:1])):
                                ins = nc.tensor.matmul(bank[4][0:1, n * P:(n + 1) * P].rearrange("o (h j) -> o h j", h=H),
                                                       column, by_head, start=True, stop=True)
                            ins.then_inc(chunk_rows, 1)
                        if q == 2:
                            pe.wait_ge(carry_ready, before + 1)
                            for n in range(2):
                                ins = nc.tensor.matmul(bank[4][:, n:n + 1], carry_rows[0:1, n].rearrange("o j h -> o (j h)"),
                                                       ones[0:1, 0:1], start=True, stop=True)
                            ins.then_inc(carry_T, 1)
                        if q == 3:
                            pe.wait_ge(max_ready, before + 1)
                            for n in range(PER_CHUNK):
                                ins = nc.tensor.transpose(bank[3][:, n * P:(n + 1) * P], edge_max[:, n * P:(n + 1) * P], ident[:, :])
                            ins.then_inc(max_T, 1)

                pe.wait_ge(q_split, NTILES * (l + 1))
                turn(0, 0, 0)
                turn(0, 0, 1)
                fetch_q(0, 0, 0, slot_tiles(0, 0))
                block_of(0, 0)
                block_of(1, 1)
                block_of(2, 0)
                with pe.Fori(1, NBLOCKS // 2 - 1) as i:
                    block_of(2 * i + 1, 1)
                    block_of(2 * i + 2, 0)
                block_of(NBLOCKS - 1, 1)
                block_of(NBLOCKS, 0)
                for q in range(FIRST_SUMMED):
                    sum_quad(*late_quad(NBLOCKS + 1, 1, q, FIRST_SUMMED))

            typed(0)
            for l in range(L):
                build_table(l)
                attend(l)
                typed(l + 1)

        @block.vector
        def _(dve):
            v = nc.vector
            chain = Chain(dve, dve_chain)

            def link(instruction):
                chain.step(instruction)
                chain.wait()

            def split_relations(l):
                link(v.tensor_scalar(rel_pri[:, l], rel_pri[:, l], HS ** -0.5, None, ALU.mult))
                att = rel_f[:, l, 0:RT * HS].rearrange("p (t o) -> p t o", o=HS)
                link(v.tensor_tensor(att, att, bc(rel_pri[:, l], 2, HS), ALU.mult))
                both = rel_f[:, l].rearrange("p (k n) -> p k n", k=2)
                left = rel_r.rearrange("p (k n) -> p k n", k=2)
                link(v.tensor_copy(rel_p[:, l, :, 0, :], both))
                link(v.tensor_tensor(left, both, rel_p[:, l, :, 0, :], ALU.subtract))
                link(v.tensor_copy(rel_p[:, l, :, 1, :], left))
                link(v.tensor_tensor(left, left, rel_p[:, l, :, 1, :], ALU.subtract))
                v.tensor_copy(rel_p[:, l, :, 2, :], left).then_inc(rel_split, 1)

            v.memset(nt_i, NT)
            v.memset(src_i, 0)
            v.memset(typ_i, 0)
            v.memset(dst_i, int(NO_DST))
            v.memset(no_node, int(NO_NODE))
            v.memset(zeros, 0.0)
            v.memset(pad_dst, NO_DST)
            v.memset(pad_key, 0.0)
            v.memset(before_first, -1.0).then_inc(pads_set, 1)
            v.memset(ones[:, :], 1.0)
            v.memset(minus_half[:, :, :], -0.5)
            v.memset(keep, 1.0)
            v.memset(carry_in[0:1, :, :, :, :], -BIG)
            dve.wait_ge(pool_const, 4)
            v.tensor_copy(iota_free[:, :], iota_i)
            link(v.tensor_copy(part_f, part_i))
            v.memset(keep[:, :, 0:1], 0.0)
            v.tensor_scalar(identb[:, :], iota_free[:, :], part_f, None, ALU.is_equal)
            v.tensor_scalar(upper, iota_free[:, :], part_f, None, ALU.is_gt)
            link(v.tensor_scalar(ident[:, :], iota_free[:, :], part_f, None, ALU.is_equal))

            dve.wait_ge(type_in, 32)
            v.tensor_copy(type_no[:, :], iota_free[:, 0:NT])
            link(v.tensor_copy(nt_f, nt_i))
            link(v.tensor_tensor(onehot_t, bc(nt_f, 1, NT), bc(type_no[:, :], 2, NTILES), ALU.is_equal))
            flat = lambda ap: ap.rearrange("p t c -> p (t c)")
            v.tensor_tensor_scan(flat(ranks), flat(keep), flat(onehot_t), 0.0, ALU.mult, ALU.add).then_inc(counted, 1)
            dve.wait_ge(placed_psum, 1)
            link(v.tensor_scalar(tot, bank[1][:, 0:NT], 127.0, None, ALU.add))
            link(v.tensor_copy(tot_i, tot))
            link(v.tensor_single_scalar(tot_i, tot_i, 7, ALU.logical_shift_right))
            link(v.tensor_copy(tiles_t, tot_i))
            link(v.tensor_tensor_scan(first_tile, ones[:, 0:NT], tiles_t, 0.0, ALU.mult, ALU.add))
            link(v.tensor_tensor(first_tile, first_tile, tiles_t, ALU.subtract))
            link(v.scalar_tensor_tensor(base_t, first_tile, float(P), bank[0][:, 0:NT], ALU.mult, ALU.add))
            link(v.tensor_tensor(ranks, ranks, bc(base_t, 2, NTILES), ALU.add))
            link(v.tensor_tensor(ranks, ranks, onehot_t, ALU.mult))
            v.tensor_reduce(is_pad, onehot_t.rearrange("p t c -> p c t"), AX.X, ALU.add)
            link(v.tensor_reduce(pos, ranks.rearrange("p t c -> p c t"), AX.X, ALU.add))
            link(v.tensor_scalar(pos, pos, -1.0, 0.0, ALU.add, ALU.max))
            link(v.tensor_copy(pos_i, pos))
            v.tensor_single_scalar(pos_lo, pos_i, P - 1, ALU.bitwise_and)
            link(v.tensor_single_scalar(pos_hi, pos_i, 7, ALU.logical_shift_right))
            v.tensor_copy(pos_lof, pos_lo)
            link(v.tensor_copy(pos, pos_hi))
            link(v.scalar_tensor_tensor(pos, pos_lof, float(SORTED_TILES), pos, ALU.mult, ALU.add))
            link(v.tensor_scalar(is_pad, is_pad, -100000.0, 100000.0, ALU.mult, ALU.add))
            link(v.tensor_tensor(pos, pos, is_pad, ALU.add))
            v.tensor_copy(place_i, pos).then_inc(place_ready, 1)
            v.tensor_copy(tile_no, iota_free[:, 0:SORTED_TILES])
            link(v.memset(junk[:, 0:1], 0.0))
            link(v.tensor_tensor(type_cmp, bc(tile_no, 2, NT), bc(first_tile, 1, SORTED_TILES), ALU.is_ge))
            link(v.tensor_reduce(type_f, type_cmp, AX.X, ALU.add))
            link(v.tensor_scalar(type_of_tile[:, :], type_f, -1.0, None, ALU.add))
            link(v.tensor_copy(tile_type[:, :], type_of_tile[0:1, :]))

            dve.wait_ge(edge_in, 96)
            v.scalar_tensor_tensor(key_f, src_i, float(RT), typ_i, ALU.mult, ALU.add)
            link(v.tensor_copy(dst_f, dst_i))
            link(v.memset(junk[:, 0:1], 0.0))
            v.memset(pad_lo, 0.0).then_inc(flat_ready, 1)
            for d in range(NTILES - 1):
                if d >= 2:
                    chain.wait(chain.n - 1)
                chain.step(v.tensor_scalar((junk, junk_b)[d % 2], dst_f, float(P * (d + 1)), None, ALU.is_lt, ALU.add,
                                           accum_out=bounds[:, d:d + 1]))
            chain.wait()
            v.memset(pad_lo, 0.0).then_inc(bound_counted, 1)
            dve.wait_ge(rel_in, 16 * 3 * H * L)
            for l in range(L):
                if l:
                    dve.wait_ge(rel_split, l)
                split_relations(l)
            dve.wait_ge(bound_psum, 1)
            link(v.tensor_copy(starts_i, bank[2][:, 0:NTILES - 1]))
            link(v.tensor_single_scalar(starts_i, starts_i, 7, ALU.logical_shift_right))
            link(v.tensor_copy(starts, starts_i))
            link(v.scalar_tensor_tensor(starts, starts, 1.0, iota_free[:, 0:NTILES - 1], ALU.add, ALU.add))
            link(v.tensor_copy(slot_no, slot_i))
            link(v.tensor_tensor(slot_cmp, bc(slot_no, 2, NTILES - 1), bc(starts, 1, SCOLS), ALU.is_ge))
            link(v.tensor_reduce(slot_dt, slot_cmp, AX.X, ALU.add))
            link(v.tensor_tensor(slot_et, slot_no, slot_dt, ALU.subtract))
            link(v.tensor_scalar(slot_et, slot_et, float(EROWS - 1), None, ALU.min))
            v.tensor_scalar(slot_base, slot_dt, float(P), None, ALU.mult)
            v.tensor_copy(slot_et_i, slot_et).then_inc(slot_rows_ready, 1)
            dve.wait_ge(place_loaded, 16)
            link(v.tensor_copy(node_f, scatter_node[:, :]))
            link(v.tensor_scalar(node_f, node_f, float(N - 1), None, ALU.min))
            v.tensor_copy(gather_node[:, :], node_f).then_inc(nodes_ready, 1)
            dve.wait_ge(slot_rows_in, 16 * SCOLS)
            link(v.tensor_tensor(s_loc, srow[:, :, 1, :], bc(slot_base, 2, P), ALU.subtract))
            link(v.tensor_scalar(s_a, s_loc, 0.0, None, ALU.is_ge))
            link(v.tensor_scalar(s_valid, s_loc, float(P - 1), None, ALU.is_le))
            link(v.tensor_tensor(s_valid, s_valid, s_a, ALU.mult))
            for k in range(2):
                link(v.tensor_tensor(s_a, srow[:, :, 1, :], srow[:, :, 2 + k, :], ALU.not_equal))
                link(v.tensor_tensor(s_flag[:, k], s_a, s_valid, ALU.mult))
            link(v.tensor_tensor(cross_col, s_valid[:, :, 0], s_flag[:, 0, :, 0], ALU.subtract))
            link(v.scalar_tensor_tensor(slot_no, s_loc[:, :, 0], 1.0, cross_col, ALU.add, ALU.mult))
            link(v.tensor_scalar(cross_col, slot_no, -1.0, None, ALU.add))
            link(v.tensor_scalar(s_flag, s_flag, -BIG, None, ALU.mult))
            v.tensor_scalar(s_valid, s_valid, BIG, -BIG, ALU.mult, ALU.add).then_inc(slot_calc, 1)
            for c in range(SCOLS):
                cols = slice(c * P, (c + 1) * P)
                dve.wait_ge(slot_T, c + 1)
                v.tensor_copy(key_of[:, cols], bank[7][:, 0:P])
                v.tensor_scalar(minus_dst[:, cols], bank[7][:, P:2 * P], -1.0, None, ALU.mult)
                v.tensor_copy(invalid[:, cols], bank[7][:, 2 * P:3 * P])
                v.tensor_copy(crossing[:, c * (P // BLOCK):(c + 1) * (P // BLOCK)],
                              bank[7][0:1, 3 * P:4 * P].rearrange("o (b s) -> o b s", s=BLOCK)[:, :, 0])
                v.tensor_copy(dst_tile[:, cols], bank[1][0:1, 0:P]).then_inc(slot_copied, 1)
            dve.wait_ge(slot_copied, SCOLS)
            dve.wait_ge(flags_stored, 32)
            v.memset(junk[:, 0:1], 0.0).then_inc(prep_done, 1)

            def layer_constants(l):
                dve.wait_ge(alpha_exp, l + 1)
                link(v.tensor_scalar(alpha_t[:, :], alpha_t[:, :], 1.0, None, ALU.add))
                v.tensor_tensor(tile_is_type, bc(type_of_tile[:, :], 2, NT), bc(type_no[:, :], 1, SORTED_TILES), ALU.is_equal)
                link(v.reciprocal(alpha_t[:, :], alpha_t[:, :]))
                link(v.tensor_tensor(tile_is_type, tile_is_type, bc(alpha_t[:, :], 1, SORTED_TILES), ALU.mult))
                link(v.tensor_reduce(half_alpha[:, :], tile_is_type, AX.X, ALU.add))
                link(v.tensor_scalar(one_less_alpha[:, :], half_alpha[:, :], -1.0, 1.0, ALU.mult, ALU.add))
                link(v.tensor_scalar(half_alpha[:, :], half_alpha[:, :], 0.5, None, ALU.mult))
                v.memset(step_mark[:, :], 0.0).then_inc(layer_const_ready, 1)

            def statistics(par, kind, tiles, mean_var_, ready):
                for t in range(GROUP):
                    chain.step(v.bn_stats(bn_in[:, par, t, :], tiles(t)))
                chain.wait()
                dve.sem_inc(passed, 1)
                for t in range(GROUP):
                    chain.step(v.bn_aggr(mean_var_[:, par, t, :], bn_in[:, par, t, :]))
                chain.wait()
                v.tensor_scalar(var_eps[:, par, kind], mean_var_[:, par, :, 1], EPS, None, ALU.add).then_inc(ready, 1)

            def typed(ph):
                if ph > 0:
                    layer_constants(ph - 1)

                def combine(i, par):
                    g = 2 * i + par
                    z = bank[Z_BANK[par]][:, :].rearrange("p (t d) -> p t d", t=GROUP)
                    hh, res = g_h[:, par], g_res[:, par]
                    wait(dve, hn_ready, g + ((ph - 1) * GROUPS - 1))
                    dve.wait_ge(tanh_done, g + ((ph - 1) * GROUPS + 1))
                    v.scalar_tensor_tensor(hh, g_th[:, par], 1.0, z, ALU.add, ALU.mult).then_inc(z_used, 1)
                    dve.wait_ge(z_used, g + ((ph - 1) * GROUPS + 1))
                    dve.wait_ge(res_scaled, g + ((ph - 1) * GROUPS + 1))
                    for t in range(GROUP):
                        chain.step(v.scalar_tensor_tensor(hh[:, t], hh[:, t], half_alpha[:, bass.ds(g * GROUP + t, 1)], res[:, t],
                                                          ALU.mult, ALU.add))
                    chain.wait()
                    statistics(par, 0, lambda t: hh[:, t], mean_var, var_ready)

                def centre(i, par):
                    g = 2 * i + par
                    hh, hn = g_h[:, par], g_hn[:, par]
                    dve.wait_ge(rstd_ready, g + ((ph - 1) * GROUPS + 1))
                    for t in range(GROUP):
                        chain.step(v.tensor_scalar(hh[:, t], hh[:, t], mean_var[:, par, t, 0:1], rstd[:, par, 0, t:t + 1],
                                                   ALU.subtract, ALU.mult))
                    chain.wait()
                    link(v.tensor_tensor(hh, hh, bc(row_const[:, 0, :], 1, GROUP), ALU.mult))
                    wait(dve, hnT_psum, g + (ph * GROUPS - 1))
                    wait(dve, stored[par], 16 * i + 16 * HALF_GROUPS if ph == 1 else 32 * HALF_GROUPS)
                    v.tensor_tensor(hn, hh, bc(row_const[:, 1, :], 1, GROUP), ALU.add).then_inc(hn_ready, 1)

                def output_statistics(i, par):
                    dve.wait_ge(out_psum, 2 * i + (2 * GROUPS + par + 1))
                    statistics(par, 1, lambda t: bank[OUT_BANK[par]][:, t * D:(t + 1) * D], out_mean_var, out_var_ready)

                def output_shift(i, par):
                    g = 2 * i + par
                    dve.wait_ge(rstd_ready, g + (GROUPS + 3))
                    dve.wait_ge(out_ready, g + (2 * GROUPS - 1))
                    v.scalar_tensor_tensor(out_shift[:, par], out_mean_var[:, par, :, 0], -1.0, rstd[:, par, 1],
                                           ALU.mult, ALU.mult).then_inc(norm_ready, 1)

                def groups(i):
                    for par in range(2):
                        coming, following, before = shifted(i, par, 2), shifted(i, par, 1), shifted(i, par, -1)
                        if is_pair(coming[0]):
                            combine(*coming)
                        if ph == 2 and is_pair(before[0]):
                            output_shift(*before)
                        if is_pair(following[0]):
                            centre(*following)
                        if ph == 2:
                            output_statistics(i, par)

                if ph > 0:
                    combine(0, 0)
                    combine(0, 1)
                    centre(0, 0)
                    repeat(dve, HALF_GROUPS - 2, groups, chain)
                    for i in (HALF_GROUPS - 2, HALF_GROUPS - 1):
                        groups(i)
                if ph == 2:
                    output_shift(HALF_GROUPS - 1, 1)

            def build_table(l):
                def tile(i, k):
                    c = 4 * i + k
                    par = k % 2
                    q0, q1, q2 = kvq[:, k, 0:D], resid1[:, 0:D], resid2[:, 0:D]
                    qp = [q_parts[:, bass.ds(c, 1), n, :].rearrange("p c d -> p (c d)") for n in range(3)]
                    dve.wait_ge(kvq_in[k], 16 * i + 16 * kvq_uses(l, 0, k) + 16)
                    link(v.tensor_copy(qp[0], q0))
                    link(v.tensor_tensor(q1, q0, qp[0], ALU.subtract))
                    link(v.tensor_copy(qp[1], q1))
                    link(v.tensor_tensor(q2, q1, qp[1], ALU.subtract))
                    v.tensor_copy(qp[2], q2).then_inc(q_split, 1)
                    wait(dve, table_stored[par], 32 * i + 16 * stage_uses(l, 0, k))
                    for n in range(1, 2 * H, 2):
                        dve.wait_ge(table_psum, 16 * c + (16 * l * NTILES + n + 1))
                        v.tensor_copy(stage[:, par, :, n * HS:(n + 1) * HS],
                                      bank[2 + n % 6][:, :].rearrange("p (t o) -> p t o", t=RT)).then_inc(stage_dve, 1)

                def four(i):
                    for k in range(4):
                        tile(i, k)

                repeat(dve, FOURS, four, chain)
                tile(FOURS, 0)

            def attend(l):
                def multiply(b, par, q):
                    quad = b * QPB + (l * NQUADS + q)
                    dve.wait_ge(rows_in[q], 64 * b + 64 * (l * NBLOCKS + 1))
                    dve.wait_ge(q_psum, quad + 1)
                    v.tensor_tensor(prod[:, q % 2], bank[1 + q % 2][:, :].rearrange("p (s d) -> p s d", s=QUAD),
                                    rows[:, par, q * QUAD:(q + 1) * QUAD, 0:D], ALU.mult).then_inc(prod_ready, 1)

                def head_sums(b, par, q):
                    quad = b * QPB + (l * NQUADS + q)
                    dve.wait_ge(prod_ready, quad + 1)
                    v.tensor_reduce(score[:, par, q * QUAD:(q + 1) * QUAD, :], prod[:, q % 2].rearrange("p s (h o) -> p s h o", h=H),
                                    AX.X, ALU.add).then_inc(score_ready, 1)

                def weigh(b, par, q):
                    part = rows[:, par, q * QUAD:(q + 1) * QUAD, :]
                    msg = part[:, :, D:2 * D].rearrange("p s (h o) -> p s h o", h=H)
                    dve.wait_ge(exp_ready, 2 * b + (2 * l * NBLOCKS + 1))
                    v.tensor_tensor(msg, msg, bc(part[:, :, RHS0:D], 3, HS), ALU.mult).then_inc(weighted, 1)

                def slot_tiles(b, q):
                    _, tiles = nc.values_load_multi_w_load_instructions(
                        dst_tile[0:1, bass.ds(b * BLOCK + q * QUAD, QUAD)], engines=[DVE_], min_val=0,
                        max_val=NTILES - 1, skip_runtime_bounds_check_because="a count of comparisons with 48 tile numbers")
                    return tiles

                def add(b, q, n, tiles):
                    quad = b * QPB + (l * NQUADS + q)
                    dve.wait_ge(sum_psum, 2 * quad + (n // 2 + 1))
                    wait(dve, sum_added, 4 * quad + n)
                    total = sums[:, bass.ds(tiles[n], 1), :].rearrange("p a n -> p (a n)")
                    v.tensor_tensor(total, total, bank[5 + n // 2][:, (n % 2) * SUMC:(n % 2 + 1) * SUMC],
                                    ALU.add).then_inc(sum_added, 1)

                def scale_crossing(b, tiles):
                    dve.wait_ge(rescale_psum, b + (l * NBLOCKS + 1))
                    link(v.tensor_scalar(rescale[:, :], bank[4][:, 0:H], 1.0, None, ALU.add))
                    wait(dve, sum_added, b * BLOCK + l * NQUADS * QUAD)
                    total = sums[:, bass.ds(tiles[0], 1), :].rearrange("p a n -> p (a n)")
                    chain.step(v.tensor_tensor(total[:, 0:H], total[:, 0:H], rescale[:, :], ALU.mult))
                    messages = total[:, H:SUMC].rearrange("p (h o) -> p h o", h=H)
                    link(v.tensor_tensor(messages, messages, bc(rescale[:, :], 2, HS), ALU.mult))

                def find_maxima(b, old, pair, q, place):
                    before = b + (l * NBLOCKS - 1)
                    if (q, place) == (0, 0):
                        dve.wait_ge(score_ready, b * QPB + l * NQUADS)
                        v.tensor_tensor(masked[:, :].rearrange("p i j h -> p j i h"), score[:, old].rearrange("p (j i) h -> p j i h", i=PER_CHUNK),
                                        bc(invalid[:, bass.ds(b * BLOCK - BLOCK, BLOCK)].rearrange("p (j i) -> p j i", i=PER_CHUNK), 3, H),
                                        ALU.add).then_inc(masked_ready, 1)
                    if (q, place) == (0, 1):
                        dve.wait_ge(flags_in[old], pair * 32 + 32 * (l * NBLOCKS // 2 + 1))
                        chain.step(v.tensor_tensor_scan(first_seg[:, :], flags[:, old, 0, :], flags[:, old, 0, :], 0.0, ALU.min, ALU.min))
                    if (q, place) == (0, 3):
                        chain.step(v.tensor_tensor_scan(last_seg[:, ::-1], flags[:, old, 1, ::-1], flags[:, old, 1, ::-1], 0.0, ALU.min, ALU.min))
                    if (q, place) == (1, 0):
                        dve.wait_ge(masked_T, before + 1)
                        chain.step(v.tensor_tensor_scan(fwd[:, :], flags[:, old, 0, :], bank[3][:, 0:CLEN], -BIG, ALU.add, ALU.max))
                    if (q, place) == (1, 1):
                        chain.wait()
                        v.tensor_tensor_scan(bwd[:, ::-1], flags[:, old, 1, ::-1], fwd[:, ::-1], -BIG, ALU.add, ALU.max).then_inc(scans_ready, 1)
                    if (q, place) == (2, 0):
                        dve.wait_ge(chunk_rows, before + 1)
                        got = bank[4][0:1, :].rearrange("o (k h j) -> o k h j", k=4, h=H)
                        for n in range(2):
                            at = 1 - n
                            chain.step(v.tensor_copy(carry_in[0:1, n, :, :, at:at + CHUNKS], got[:, 2 * n:2 * n + 2]))
                        chain.step(v.tensor_copy(carry_in[0:1, 0, 0, :, 0], carried[:, :]))
                    if (q, place) == (2, 1):
                        row = lambda ap: ap.rearrange("o h j -> o (h j)")
                        chain.wait()
                        chain.step(v.tensor_tensor_scan(row(carry_out[0:1, 0]), row(carry_in[0:1, 0, 1]), row(carry_in[0:1, 0, 0]),
                                                        -BIG, ALU.add, ALU.max))
                        chain.step(v.tensor_tensor_scan(row(carry_out[0:1, 1])[:, ::-1], row(carry_in[0:1, 1, 1])[:, ::-1],
                                                        row(carry_in[0:1, 1, 0])[:, ::-1], -BIG, ALU.add, ALU.max))
                    if (q, place) == (2, 2):
                        chain.wait()
                        chain.step(v.tensor_copy(carry_rows[0:1, 0], carry_out[0:1, 0, :, 0:CHUNKS].rearrange("o h j -> o j h")))
                        v.tensor_copy(carry_rows[0:1, 1], carry_out[0:1, 1, :, 1:CHUNKS + 1].rearrange("o h j -> o j h")
                                      ).then_inc(carry_ready, 1)
                    if (q, place) == (3, 0):
                        dve.wait_ge(carry_T, before + 1)
                        chain.step(v.tensor_copy(chunk_carry[:, :], bank[4][:, 0:2]))
                    if (q, place) == (3, 1):
                        chain.wait()
                        chain.step(v.scalar_tensor_tensor(edge_max[:, :], first_seg[:, :], chunk_carry[:, 0:1], bwd[:, :], ALU.add, ALU.max))
                    if (q, place) == (3, 2):
                        chain.wait()
                        v.scalar_tensor_tensor(edge_max[:, :], last_seg[:, :], chunk_carry[:, 1:2], edge_max[:, :], ALU.add,
                                               ALU.max).then_inc(max_ready, 1)
                    if (q, place) == (4, 0):
                        dve.wait_ge(max_T, before + 1)
                        by_half = lambda ap: ap.rearrange("p (j i) h -> p i j h", i=PER_CHUNK)
                        v.tensor_tensor(by_half(below_max[:, :, :]), masked[:, :],
                                        bank[3][:, 0:CLEN].rearrange("p (i j h) -> p i j h", i=PER_CHUNK, h=H),
                                        ALU.subtract).then_inc(below_ready, 1)
                        chain.step(v.tensor_tensor(lower[:, :], carry_in[0:1, 0, 0, :, 0], bank[3][0:1, 0:H], ALU.subtract))
                        v.tensor_copy(carried[:, :], carry_out[0:1, 0, :, CHUNKS])
                        v.tensor_scalar(cross_hot[:, :], iota_free[0:1, :], crossing[:, bass.ds(b - 1, 1)], None, ALU.is_equal)
                    if (q, place) == (4, 1):
                        chain.wait()
                        v.tensor_scalar(lower[:, :], lower[:, :], 0.0, None, ALU.min).then_inc(lower_ready, 1)
                    if (q, place) == (4, 3):
                        dve.wait_ge(exp_ready, 2 * before + 2)
                        v.tensor_scalar(lower[:, :], lower[:, :], -1.0, None, ALU.add).then_inc(cross_ready, 1)

                def step(b, par, pair, q):
                    late, weigh_next = late_quad(b, par, q, FIRST_SUMMED), late_quad(b, par, q, FIRST_WEIGHED)
                    adding, maxima = is_block(late[0]), is_block(b - 1)
                    if adding:
                        tiles = slot_tiles(late[0], late[2])
                    if is_block(b):
                        multiply(b, par, q)
                    if adding and q == FIRST_SUMMED:
                        scale_crossing(b - 1, tiles)
                    weigh_place = 0 if not is_block(b) and q != FIRST_WEIGHED else 3
                    for place in range(4):
                        if place == 0 and weigh_place == 0 and is_block(weigh_next[0]):
                            weigh(*weigh_next)
                        if adding:
                            add(late[0], late[2], place, tiles)
                        if place == 1 and is_block(b):
                            head_sums(b, par, q)
                        if place == 3 and weigh_place == 3 and is_block(weigh_next[0]):
                            weigh(*weigh_next)
                        if maxima:
                            find_maxima(b, 1 - par, pair, q, place)

                def block_of(b, par, pair):
                    for q in range(QPB):
                        step(b, par, pair, q)

                v.memset(carried[:, :], -BIG)
                dve.wait_ge(spread_ready, NTILES * (l + 1))
                if l:
                    dve.wait_ge(agg_stored, 16 * len(AGG_PARTS) * l)
                link(v.memset(sums[:, :, :], 0.0))
                block_of(0, 0, None)
                chain_start = chain.n
                block_of(1, 1, 0)
                block_of(2, 0, 0)
                per = chain.n - chain_start
                with dve.Fori(1, NBLOCKS // 2 - 1) as i:
                    chain.n = i * per + chain_start
                    block_of(2 * i + 1, 1, i)
                    block_of(2 * i + 2, 0, i)
                chain.n = chain_start + per * (NBLOCKS // 2 - 1)
                block_of(NBLOCKS - 1, 1, NBLOCKS // 2 - 1)
                block_of(NBLOCKS, 0, NBLOCKS // 2 - 1)
                for q in range(FIRST_SUMMED):
                    step(NBLOCKS + 1, 1, None, q)
                dve.wait_ge(sum_added, 4 * NQUADS * (l + 1))
                link(v.tensor_scalar(recip, sums[:, :, 0:H], 1e-30, None, ALU.max))
                link(v.reciprocal(recip, recip))
                for part in AGG_PARTS:
                    messages = sums[:, part, H:SUMC].rearrange("p c (h o) -> p c h o", h=H)
                    v.tensor_tensor(messages, messages, bc(recip[:, part], 3, HS), ALU.mult).then_inc(agg_ready, 1)

            typed(0)
            for l in range(L):
                build_table(l)
                attend(l)
                typed(l + 1)


_INS = ["x", "src", "dst", "edge_type_32", "node_type_16", "L0_gnn_Wk", "L0_gnn_Wq", "L0_gnn_Wv", "L0_gnn_Wa", "L0_gnn_Watt",
        "L0_gnn_Wmsg", "L0_gnn_pri", "L0_gnn_skip", "L0_gnn_ln_g", "L0_gnn_ln_b", "L0_gnn_ff_w", "L0_gnn_ff_b"]


def kernel(**inputs):
    import numpy as _np
    import concourse.bacc as _bacc
    from concourse import mybir as _mybir
    from concourse.bass_utils import run_bass_kernel_spmd as _run

    nc = _bacc.Bacc("TRN2", target_bir_lowering=False, num_devices=1)
    arrays, args = {}, []
    for name in _INS:
        a = _np.ascontiguousarray(inputs[name])
        arrays[f"in_{name}_dram"] = a
        args.append(nc.dram_tensor(f"in_{name}_dram", a.shape, _mybir.dt.from_np(a.dtype), kind="ExternalInput").ap())
    args.append(nc.dram_tensor("out_dram", (N, D), _mybir.dt.float32, kind="ExternalOutput").ap())
    gnn_kernel(nc, *args)
    r = _run(nc, [arrays], core_ids=[0])
    return r.results[0]["out_dram"]
```
